# Optimizing a Trainium2 kernel written in Bass

```python
import numpy as np
import jax
import jax.numpy as jnp

def _softmax(x, axis=-1):
    return jax.nn.softmax(x, axis=axis)

def _gelu(x):
    return jax.nn.gelu(x, approximate=True)

def _silu(x):
    return jax.nn.silu(x)

def _sigmoid(x):
    return jax.nn.sigmoid(x)

def _layernorm(x, axis=-1, eps=1e-05):
    m = jnp.mean(x, axis=axis, keepdims=True)
    v = jnp.var(x, axis=axis, keepdims=True)
    return (x - m) / jnp.sqrt(v + eps)

def _scatter_add(tgt, idx, src, axis=0):
    return tgt.at[idx].add(src)

def _segment_sum(src, seg, n):
    return jax.ops.segment_sum(src, seg, n)
kernel_name = 'mk_adj_preln_d4_adj_r2_977b70'

def setup_inputs(seed: int=0):
    np.random.seed(seed)
    _w = jnp.asarray

    def _rec_inputs():
        import jax
        import jax.numpy as jnp
        _gk = jax.random.key(seed)
        x = -0.000929 + 1 * jax.random.normal(jax.random.fold_in(_gk, 1), (8, 1024, 128), jnp.float32)
        _a = jax.random.bernoulli(jax.random.fold_in(_gk, 2), 0.00195312, (8, 1024, 1024))
        adj = _a.astype(jnp.int32)
        return (x, adj)
    x, adj = _rec_inputs()

    def _L0_gnn_setup():
        import jax, jax.numpy as jnp
        import numpy as np
        ALPHA = 0.2
        NEG = -9000000000000000.0
        key = jax.random.key(seed)
        ks = jax.random.split(key, 6)
        B, N, F, H, D = (16, 256, 128, 8, 32)
        x = jax.random.normal(ks[0], (B, N, F), dtype=jnp.float32)
        adj = jax.random.randint(ks[1], (B, N, N), 0, 2, dtype=jnp.int32)
        W1 = jax.random.normal(ks[2], (H, F, D), dtype=jnp.float32) * (1.414 * (6.0 / (F + D)) ** 0.5)
        a1 = jax.random.normal(ks[3], (H, 2 * D), dtype=jnp.float32) * 0.2
        W2 = jax.random.normal(ks[4], (H * D, F), dtype=jnp.float32) * (1.414 * (6.0 / (H * D + F)) ** 0.5)
        a2 = jax.random.normal(ks[5], (2 * F,), dtype=jnp.float32) * 0.2
        return {'x': x, 'adj': adj, 'W1': W1, 'a1': a1, 'W2': W2, 'a2': a2}
    _L0_gnn_all = _L0_gnn_setup()
    _L0_gnn_in = {k: v for k, v in _L0_gnn_all.items() if k in ('W1', 'a1', 'W2', 'a2')}
    del _L0_gnn_all

    def _L1_gnn_setup():
        import jax, jax.numpy as jnp
        import numpy as np
        NEG_BIG = -9000000000000000.0
        ALPHA = 0.2
        key = jax.random.key(seed)
        k1, k2, k3, k4 = jax.random.split(key, 4)
        B, N, F_in, F_out = (8, 1024, 128, 128)
        h = jax.random.normal(k1, (B, N, F_in), dtype=jnp.float32)
        adj = jax.random.randint(k2, (B, N, N), 0, 2, dtype=jnp.int32)

        def xavier(k, shape, gain=1.414):
            fan_in, fan_out = (shape[0], shape[1])
            bound = gain * np.sqrt(6.0 / (fan_in + fan_out))
            return jax.random.uniform(k, shape, jnp.float32, -bound, bound)
        W = xavier(k3, (F_in, F_out))
        a = xavier(k4, (2 * F_out, 1))
        return {'h': h, 'adj': adj, 'W': W, 'a': a}
    _L1_gnn_all = _L1_gnn_setup()
    _L1_gnn_in = {k: v for k, v in _L1_gnn_all.items() if k in ('W', 'a')}
    del _L1_gnn_all

    def _L2_gnn_setup():
        import jax, jax.numpy as jnp
        import numpy as np
        IN_DIM = 128
        OUT_DIM = 128
        B, N = (8, 1024)
        NEG_SLOPE = 0.2
        key = jax.random.key(seed)
        k_h, k_adj, k_W, k_a = jax.random.split(key, 4)
        h = jax.random.normal(k_h, (B, N, IN_DIM), dtype=jnp.float32)
        adj = jax.random.randint(k_adj, (B, N, N), 0, 2, dtype=jnp.int32)
        W = jax.random.normal(k_W, (OUT_DIM, IN_DIM), dtype=jnp.float32) * (1.0 / np.sqrt(IN_DIM))
        a = jax.random.normal(k_a, (2 * OUT_DIM,), dtype=jnp.float32) * (1.0 / np.sqrt(2 * OUT_DIM))
        return {'h': h, 'adj': adj, 'W': W, 'a': a}
    _L2_gnn_all = _L2_gnn_setup()
    _L2_gnn_in = {k: v for k, v in _L2_gnn_all.items() if k in ('W', 'a')}
    del _L2_gnn_all

    def _L3_gnn_setup():
        import jax, jax.numpy as jnp
        import numpy as np
        BN_EPS = 0.001
        NEG_INF = -1e+30

        def _masked_row_softmax(adjT):
            mask = adjT != 0
            logits = jnp.where(mask, adjT, NEG_INF)
            p = jax.nn.softmax(logits, axis=-1)
            return jnp.where(mask, p, 0.0)

        def _batch_norm(x, gamma, beta):
            mean = jnp.mean(x, axis=(0, 1), keepdims=True)
            var = jnp.var(x, axis=(0, 1), keepdims=True)
            return (x - mean) * jax.lax.rsqrt(var + BN_EPS) * gamma + beta
        key = jax.random.key(seed)
        ks = jax.random.split(key, 4)
        B, N, F = (1, 4096, 128)
        C0, C1 = (128, 128)
        features = jax.random.normal(ks[0], (B, N, F), dtype=jnp.float32)
        adj = jax.random.randint(ks[1], (B, N, N), 0, 2, dtype=jnp.int32)
        kernel_1 = jax.random.normal(ks[2], (F, C0), dtype=jnp.float32) * (1.0 / np.sqrt(F))
        kernel_2 = jax.random.normal(ks[3], (C0, C1), dtype=jnp.float32) * (1.0 / np.sqrt(C0))
        return {'features': features, 'adj': adj, 'kernel_1': kernel_1, 'bias_1': jnp.zeros((C0,), jnp.float32), 'gamma_1': jnp.ones((C0,), jnp.float32), 'beta_1': jnp.zeros((C0,), jnp.float32), 'kernel_2': kernel_2, 'bias_2': jnp.zeros((C1,), jnp.float32), 'gamma_2': jnp.ones((C1,), jnp.float32), 'beta_2': jnp.zeros((C1,), jnp.float32)}
    _L3_gnn_all = _L3_gnn_setup()
    _L3_gnn_in = {k: v for k, v in _L3_gnn_all.items() if k in ('kernel_1', 'bias_1', 'gamma_1', 'beta_1', 'kernel_2', 'bias_2', 'gamma_2', 'beta_2')}
    del _L3_gnn_all
    return {'x': x, 'adj': adj, 'L0_gnn_W1': _L0_gnn_in['W1'], 'L0_gnn_a1': _L0_gnn_in['a1'], 'L0_gnn_W2': _L0_gnn_in['W2'], 'L0_gnn_a2': _L0_gnn_in['a2'], 'L1_gnn_W': _L1_gnn_in['W'], 'L1_gnn_a': _L1_gnn_in['a'], 'L2_gnn_W': _L2_gnn_in['W'], 'L2_gnn_a': _L2_gnn_in['a'], 'L3_gnn_kernel_1': _L3_gnn_in['kernel_1'], 'L3_gnn_bias_1': _L3_gnn_in['bias_1'], 'L3_gnn_gamma_1': _L3_gnn_in['gamma_1'], 'L3_gnn_beta_1': _L3_gnn_in['beta_1'], 'L3_gnn_kernel_2': _L3_gnn_in['kernel_2'], 'L3_gnn_bias_2': _L3_gnn_in['bias_2'], 'L3_gnn_gamma_2': _L3_gnn_in['gamma_2'], 'L3_gnn_beta_2': _L3_gnn_in['beta_2']}

def reference(x, adj, L0_gnn_W1, L0_gnn_a1, L0_gnn_W2, L0_gnn_a2, L1_gnn_W, L1_gnn_a, L2_gnn_W, L2_gnn_a, L3_gnn_kernel_1, L3_gnn_bias_1, L3_gnn_gamma_1, L3_gnn_beta_1, L3_gnn_kernel_2, L3_gnn_bias_2, L3_gnn_gamma_2, L3_gnn_beta_2):
    import jax
    import jax.numpy as jnp

    def _L0_gnn_ref(x, adj, W1, a1, W2, a2):
        import jax, jax.numpy as jnp
        import numpy as np
        ALPHA = 0.2
        NEG = -9000000000000000.0
        mask = adj > 0
        h = jnp.einsum('bnf,hfd->bhnd', x, W1)
        D = h.shape[-1]
        f1 = jnp.einsum('bhnd,hd->bhn', h, a1[:, :D])
        f2 = jnp.einsum('bhnd,hd->bhn', h, a1[:, D:])
        e = jax.nn.leaky_relu(f1[..., :, None] + f2[..., None, :], ALPHA)
        e = jnp.where(mask[:, None, :, :], e, NEG)
        att = jax.nn.softmax(e, axis=-1)
        hp = jnp.einsum('bhij,bhjd->bhid', att, h)
        hp = jax.nn.elu(hp)
        B, H, N, Dh = hp.shape
        xc = hp.transpose(0, 2, 1, 3).reshape(B, N, H * Dh)
        h2 = jnp.einsum('bnk,kc->bnc', xc, W2)
        C = h2.shape[-1]
        g1 = jnp.einsum('bnc,c->bn', h2, a2[:C])
        g2 = jnp.einsum('bnc,c->bn', h2, a2[C:])
        e2 = jax.nn.leaky_relu(g1[:, :, None] + g2[:, None, :], ALPHA)
        e2 = jnp.where(mask, e2, NEG)
        att2 = jax.nn.softmax(e2, axis=-1)
        hp2 = jnp.einsum('bij,bjc->bic', att2, h2)
        return jax.nn.elu(hp2) + x

    def _L1_gnn_ref(h, adj, W, a):
        import jax, jax.numpy as jnp
        import numpy as np
        NEG_BIG = -9000000000000000.0
        ALPHA = 0.2
        Wh = jnp.einsum('bnf,fo->bno', h, W)
        F_out = W.shape[1]
        a1 = a[:F_out, 0]
        a2 = a[F_out:, 0]
        s1 = Wh @ a1
        s2 = Wh @ a2
        e = jax.nn.leaky_relu(s1[:, :, None] + s2[:, None, :], negative_slope=ALPHA)
        e = jnp.where(adj > 0, e, NEG_BIG)
        attn = jax.nn.softmax(e, axis=-1)
        h_prime = jnp.einsum('bij,bjo->bio', attn, Wh)
        return jax.nn.elu(h_prime)

    def _L2_gnn_ref(h, adj, W, a):
        import jax, jax.numpy as jnp
        import numpy as np
        IN_DIM = 128
        OUT_DIM = 128
        B, N = (8, 1024)
        NEG_SLOPE = 0.2
        Wh = jnp.einsum('bnf,of->bno', h, W)
        Fo = Wh.shape[-1]
        a_src, a_dst = (a[:Fo], a[Fo:])
        s = Wh @ a_src
        t = Wh @ a_dst
        e = jax.nn.leaky_relu(s[:, :, None] + t[:, None, :], negative_slope=NEG_SLOPE)
        e = jnp.where(adj == 0, -jnp.inf, e)
        alpha = jax.nn.softmax(e, axis=-1)
        alpha = jnp.nan_to_num(alpha, nan=0.0)
        return jnp.einsum('bnm,bmo->bno', alpha, Wh)

    def _L3_gnn_ref(features, adj, kernel_1, bias_1, gamma_1, beta_1, kernel_2, bias_2, gamma_2, beta_2):
        import jax, jax.numpy as jnp
        import numpy as np
        BN_EPS = 0.001
        NEG_INF = -1e+30

        def _masked_row_softmax(adjT):
            mask = adjT != 0
            logits = jnp.where(mask, adjT, NEG_INF)
            p = jax.nn.softmax(logits, axis=-1)
            return jnp.where(mask, p, 0.0)

        def _batch_norm(x, gamma, beta):
            mean = jnp.mean(x, axis=(0, 1), keepdims=True)
            var = jnp.var(x, axis=(0, 1), keepdims=True)
            return (x - mean) * jax.lax.rsqrt(var + BN_EPS) * gamma + beta
        adjT = jnp.transpose(adj.astype(jnp.float32), (0, 2, 1))
        w = _masked_row_softmax(adjT)
        region = jnp.matmul(w, features)
        region = jnp.matmul(region, kernel_1) + bias_1
        region = _batch_norm(region, gamma_1, beta_1)
        people = jnp.matmul(jnp.transpose(w, (0, 2, 1)), region)
        people = jnp.matmul(people, kernel_2) + bias_2
        people = _batch_norm(people, gamma_2, beta_2)
        return people
    h = jnp.maximum(_layernorm(x, axis=-1), 0.0)
    x = x + _L0_gnn_ref(h, adj, L0_gnn_W1, L0_gnn_a1, L0_gnn_W2, L0_gnn_a2)
    h = jnp.maximum(_layernorm(x, axis=-1), 0.0)
    x = x + _L1_gnn_ref(h, adj, L1_gnn_W, L1_gnn_a)
    h = jnp.maximum(_layernorm(x, axis=-1), 0.0)
    x = x + _L2_gnn_ref(h, adj, L2_gnn_W, L2_gnn_a)
    h = jnp.maximum(_layernorm(x, axis=-1), 0.0)
    x = x + _L3_gnn_ref(h, adj, L3_gnn_kernel_1, L3_gnn_bias_1, L3_gnn_gamma_1, L3_gnn_beta_1, L3_gnn_kernel_2, L3_gnn_bias_2, L3_gnn_gamma_2, L3_gnn_beta_2)
    return x

_drawn_inputs = setup_inputs


def setup_inputs(seed=0):
    import zlib

    import numpy as np

    out = dict(_drawn_inputs(seed))
    spreads = {'L3_gnn_bias_1': (0.0, 0.8),
     'L3_gnn_gamma_1': (1.0, 0.2),
     'L3_gnn_beta_1': (0.0, 0.452),
     'L3_gnn_bias_2': (0.0, 0.8),
     'L3_gnn_gamma_2': (1.0, 0.2),
     'L3_gnn_beta_2': (0.0, 0.278)}
    factors = {'L2_gnn_a': 4.635}
    for name, (base, spread) in spreads.items():
        noise = np.random.default_rng([zlib.crc32(name.encode()), seed]).standard_normal(out[name].shape)
        drawn = base * np.exp(spread * noise) if base else spread * noise
        out[name] = jnp.asarray(drawn.astype(out[name].dtype))
    for name, factor in factors.items():
        out[name] = (out[name] * factor).astype(out[name].dtype)
    return out
```

```python
from contextlib import ExitStack

import concourse.bass as bass
from concourse import mybir

F32 = mybir.dt.float32
BF16 = mybir.dt.bfloat16
FP8 = mybir.dt.float8e4
I32 = mybir.dt.int32
U32 = mybir.dt.uint32
U8 = mybir.dt.uint8
ALU = mybir.AluOpType
ACT = mybir.ActivationFunctionType
AX_X = mybir.AxisListType.X
RMAX = bass.bass_isa.ReduceOp.max

P = 128
SLOPE = 0.2
LN_EPS = 1e-5
BN_EPS = 1e-3
STEP_GAIN = 1e30

PER = dict(
    ln_var=4, rstd=4, nmr=4, h_ready=8, gen_full=62, gen_free=62, csum=3, mean_lhs=3,
    f2_range=4, f2_gmax=4, args=4, exps=4, v_full=5, v_hi=6, v_rest=6, v_mid=6, v_ready=6,
    bcast=11, act_cmp=11, mplus=11, mminus=3, m_used=11, slot_full=56, act_slot=48, dve_slot=32,
    mneg=3, eexp=3, xc_ready=1, x1_ready=1, x3_ready=1, region=1, stats=1,
    adj_conv=8, at_full=8, at_ready=8, pe_done=1, dve_done=1,
)
DVE_STEPS = 300


def adjacency_gnn_stack(nc, x, adj, W1, a1, W2, a2, gW, ga, lW, la, K1, b1, gam1, bet1, K2, b2, gam2, bet2, out):
    B, N, F = x.shape
    H, _, D = W1.shape
    NT = N // P
    HD = H * D
    E = D + 1
    E1 = F + 1
    C0 = HD + 2 * H
    C1 = F + 2
    HALF = N // 2
    DVE_CMP = 5
    assert F == P and N == 1024 and B % 2 == 0 and H == 8

    with ExitStack() as ctx:
        def sb(name, shape, dt):
            return ctx.enter_context(nc.sbuf_tensor(name, shape, dt))

        def pb(name, shape, dt):
            return ctx.enter_context(nc.psum_tensor(name, shape, dt))

        def sem(name):
            return ctx.enter_context(nc.semaphore(name))

        GT = sb("GT", [P, B * N], F32)
        adj_in = sb("adj_in", [P, 2, N], I32)
        A = sb("A", [P, 2, NT, N], BF16)
        AT = sb("AT", [P, 2, NT, N], FP8)
        M = sb("M", [P, 2, NT, N], FP8)
        Fb = sb("Fb", [P, 2, N], F32)
        V = sb("V", [P, NT * H * 3 * 2 * E], BF16)
        Vf = sb("Vf", [P, NT * H * 2 * E], F32)
        Dn = sb("Dn", [P, NT * H * E], F32)
        Hn = sb("Hn", [P, NT * C0], F32)
        rows = sb("rows", [P, 2, N], F32)
        H0 = sb("H0", [P, NT, F], F32)
        xin = sb("xin", [P, NT, F], F32)
        xw = sb("xw", [P, NT, F], F32)
        WX0 = sb("WX0", [P, C0], F32)
        WR0 = sb("WR0", [P, 2, P], F32)
        WX1 = sb("WX1", [P, 2, C1], F32)
        WX2 = sb("WX2", [P, C1], F32)
        WX3 = sb("WX3", [P, C1], F32)
        K1s = sb("K1s", [P, F], F32)
        K2s = sb("K2s", [P, F], F32)
        b1b = sb("b1b", [P, F], F32)
        cols = sb("cols", [P, 8], F32)
        ident = sb("ident", [P, P], F32)
        identb = sb("identb", [P, P], BF16)
        ones = sb("ones", [P, P], F32)
        mhalf = sb("mhalf", [P, NT], F32)
        meanb = sb("meanb", [P, HD], F32)
        mean_lhs = sb("mean_lhs", [P, 2, P], F32)
        csum = sb("csum", [P, 4], F32)
        st6 = sb("st6", [P, NT, 6], F32)
        mv = sb("mv", [P, NT, 2], F32)
        ve = sb("ve", [P, NT], F32)
        rstd = sb("rstd", [P, NT], F32)
        nmr = sb("nmr", [P, NT], F32)
        f2r = sb("f2r", [P, 2 * H], F32)
        f2g = sb("f2g", [P, 2 * H], F32)
        Cb = sb("Cb", [P, H], F32)
        nf2 = sb("nf2", [P, NT * H], F32)
        bigf2 = sb("bigf2", [P, NT * H], F32)
        sarg = sb("sarg", [P, NT * H], F32)
        args = sb("args", [P, 4, NT * H], F32)
        fac = sb("fac", [P, 4, NT * H], F32)
        rden = sb("rden", [P, NT * H], F32)
        Tm = sb("Tm", [P, 2, E1], F32)
        deg = sb("deg", [P, 2, NT], F32)
        cnt = sb("cnt", [P, 2, NT], F32)
        emp = sb("emp", [P, NT], F32)
        rc = sb("rc", [P, NT], F32)
        rcr = sb("rcr", [P, NT], F32)
        rc3 = sb("rc3", [P, NT, 3], BF16)
        q3 = sb("q3", [P, NT, 3], F32)
        Qall = sb("Qall", [P, B * NT], F32)
        bnacc = sb("bnacc", [P, 2], F32)
        sc = sb("sc", [P, 16], F32)
        tK2 = sb("tK2", [1, F], F32)
        qT = sb("qT", [B * NT, P], F32)
        bst = sb("bst", [P, B * N // 512, 6], F32)
        x3_dram = nc.dram_tensor("x3_dram", (B * N, F), F32).ap()

        gen = pb("gen", [P, 2, 512], F32)
        mps = pb("mps", [P, 4, 512], F32)
        tps = pb("tps", [P, N], BF16)
        sps = pb("sps", [P, 512], F32)

        S = {k: sem(k) for k in PER}
        dve_chain = sem("dve_chain")
        adj_land = [sem("adj_land0"), sem("adj_land1")]
        x_land, x3_store = sem("x_land"), sem("x3_store")
        w_land, w_pool, w_dve, w_pe, w_act = sem("w_land"), sem("w_pool"), sem("w_dve"), sem("w_pe"), sem("w_act")
        t_dve, t_pe, t_act, t_pool, t_ld, t_out = (sem("t_dve"), sem("t_pe"), sem("t_act"), sem("t_pool"),
                                                   sem("t_ld"), sem("t_out"))
        t_x3, t_free = sem("t_x3"), sem("t_free")
        t_gf, t_ge = sem("t_gf"), sem("t_ge")

        hT = Dn[:, 0:N]
        V0 = V[:, :].rearrange("p (t h q c) -> p t h q c", t=NT, h=H, q=3)
        V1 = V[:, 0:NT * 3 * 2 * E1].rearrange("p (t q c) -> p t q c", t=NT, q=3)
        V3 = V[:, 0:NT * 3 * F].rearrange("p (t q c) -> p t q c", t=NT, q=3)
        Vf0 = Vf[:, :].rearrange("p (t h c) -> p t h c", t=NT, h=H)
        Vf1 = Vf[:, 0:NT * 2 * E1].rearrange("p (t c) -> p t c", t=NT)
        Vf3 = Vf[:, 0:NT * F].rearrange("p (t c) -> p t c", t=NT)
        xcT = Vf[:, 0:2 * N].rearrange("p (k n) -> p k n", k=2)
        D0 = Dn[:, :].rearrange("p (t h c) -> p t h c", t=NT, h=H)
        D1 = Dn[:, 0:NT * E1].rearrange("p (t c) -> p t c", t=NT)
        D3 = Dn[:, 0:NT * F].rearrange("p (t c) -> p t c", t=NT)
        Hn0 = Hn[:, :].rearrange("p (t c) -> p t c", t=NT)
        Hn1 = Hn[:, 0:NT * C1].rearrange("p (t c) -> p t c", t=NT)
        xc = Hn[:, 0:NT * HD].rearrange("p (t c) -> p t c", t=NT)
        sq3 = Hn[:, 0:NT * F].rearrange("p (t c) -> p t c", t=NT)

        def thin(view):
            return view.rearrange("p t h c -> p (t h) c")

        def thin_v(layer):
            if layer == 0:
                return V[:, :].rearrange("p (n q c) -> p n q c", q=3, c=2 * E)
            return V1

        def thin_f(layer):
            if layer == 0:
                return Vf[:, :].rearrange("p (n c) -> p n c", c=2 * E)
            return Vf1

        GEN = {0: 0, 1: 15, 2: 30, 3: 43, 4: 55}
        NTR = {0: 2, 1: 4, 2: 2, 3: 2, 4: 2}
        SLOT = {0: 0, 1: 24, 2: 32, 3: 40, 4: 48}
        LN = {0: 0, 2: 1, 3: 2, 4: 3}
        PAIRS = B // 2

        def upto(pair, half, name, k):
            return pair * (2 * PER[name]) + (half * PER[name] + k)

        LOADS = 16

        passed = {e: sem("passed_" + e) for e in ("pe", "act", "dve", "pool")}

        def alone(eng, name):
            eng.sem_inc(passed[name], 1)

        block = ctx.enter_context(nc.Block())

        @block.sync
        def _(sp):
            col = lambda v: v.rearrange("(c o) -> c o", o=1)
            row = lambda v, n: v.rearrange("(o n) -> o n", o=1).to_broadcast([P, n])
            loads = [
                (WX0[:, 0:HD].rearrange("f (h d) -> f h d", h=H), W1.rearrange("h f d -> f h d")),
                (Fb[:, 0, 0:2 * HD], a1.rearrange("(o h) d -> o (h d)", o=1).to_broadcast([P, 2 * HD])),
                (WX1[:, :, 0:F], W2.rearrange("(k p) c -> p k c", p=P)),
                (Fb[:, 1, 0:2 * F], row(a2, 2 * F)),
                (WX2[:, 0:F], gW),
                (Fb[:, 1, 2 * F:4 * F], ga.rearrange("n o -> o n").to_broadcast([P, 2 * F])),
                (H0[:, 0, :], lW),
                (Fb[:, 0, 2 * HD:2 * HD + 2 * F], row(la, 2 * F)),
                (K1s[:, :], K1), (K2s[:, :], K2), (b1b[:, :], row(b1, F)),
                (cols[:, 0:1], col(gam1)), (cols[:, 1:2], col(bet1)), (cols[:, 2:3], col(b2)),
                (cols[:, 3:4], col(gam2)), (cols[:, 4:5], col(bet2)),
            ]
            for dst, src in loads:
                sp.dma_start(dst, src).then_inc(w_land, 16)
            sp.dma_start(xin[:, :, :], x[0].rearrange("(t p) f -> p t f", p=P)).then_inc(x_land, 16)
            for t in range(NT):
                if t >= 2:
                    sp.wait_ge(S["adj_conv"], t - 1)
                sp.dma_start(adj_in[:, t % 2, :], adj[0, t * P:(t + 1) * P, :]).then_inc(adj_land[t % 2], 16)
            adj_rows = adj.rearrange("b n m -> (b n) m")
            x_rows = x.rearrange("b n f -> (b n) f")
            with sp.Fori(0, PAIRS) as pair:
                following = [pair * (2 * N) + N,
                             sp.snap((pair * (2 * N) + 2 * N) % (B * N), min_val=0, max_val=(B - 1) * N)]
                for half in range(2):
                    nxt = following[half]
                    for t in range(NT):
                        sp.wait_ge(S["adj_conv"], upto(pair, half, "adj_conv", NT + t - 1))
                        sp.dma_start(adj_in[:, t % 2, :], adj_rows[bass.ds(nxt + t * P, P), :])\
                            .then_inc(adj_land[t % 2], 16)
                    sp.wait_ge(S["x1_ready"], upto(pair, half, "x1_ready", 1))
                    sp.dma_start(xin[:, :, :], x_rows[bass.ds(nxt, N), :].rearrange("(t p) f -> p t f", p=P))\
                        .then_inc(x_land, 16)
                    sp.wait_ge(S["x3_ready"], upto(pair, half, "x3_ready", 1))
                    sp.dma_start(x3_dram[bass.ds(pair * (2 * N) + half * N, N), :]
                                 .rearrange("(t p) f -> p t f", p=P), xw[:, :, :]).then_inc(x3_store, 16)
            sp.wait_ge(x3_store, 16 * B)
            X3 = A[:, :, :, :].rearrange("p a t n -> p (a t n)").bitcast(F32).rearrange("p (t f) -> p t f", f=F)
            sp.wait_ge(t_free, 1)
            sp.dma_start(X3, x3_dram.rearrange("(t p) f -> p t f", p=P)).then_inc(t_x3, 16)
            sp.wait_ge(t_act, 1)
            qrow = [M, AT]
            for k in range(2):
                dst = qrow[k][0:1, :, :, :].rearrange("o a t n -> o (a t n)").bitcast(F32)
                sp.dma_start(dst.rearrange("o (k n) -> o k n", n=P), qT[k * 32:(k + 1) * 32, :]).then_inc(t_ld, 16)
            o_rows = out.rearrange("b n f -> (b n) f").rearrange("(g t p) f -> g p t f", p=P, t=4)
            for g in range(B * N // 512):
                sp.wait_ge(t_out, g + 1)
                sp.dma_start(o_rows[g], X3[:, 4 * g:4 * g + 4, :]).then_inc(t_x3, 16)
            sp.wait_ge(t_x3, 16 * (1 + B * N // 512))

        @block.gpsimd
        def _(pool):
            nc.gpsimd.memset(ident[:, :], 0.0).then_inc(w_pool, 1)
            nc.gpsimd.memset(ones[:, :], 1.0).then_inc(w_pool, 1)
            nc.gpsimd.memset(mhalf[:, :], -0.5).then_inc(w_pool, 1)
            pool.wait_ge(w_pool, 3)
            nc.gpsimd.affine_select(out=ident[:, :], in_=ident[:, :], compare_op=ALU.not_equal, fill=1.0,
                                    base=0, pattern=[[-1, P]], channel_multiplier=1).then_inc(w_pool, 1)
            pool.wait_ge(w_pool, 4)

            with pool.Fori(0, PAIRS) as pair:
                for half in range(2):
                    def wait(name, k):
                        pool.wait_ge(S[name], upto(pair, half, name, k))
                        alone(pool, "pool")

                    for layer in range(5):
                        if layer in LN:
                            wait("ln_var", LN[layer] + 1)
                            nc.gpsimd.tensor_tensor(rstd[:, :], ve[:, :], mhalf[:, :], ALU.pow).then_inc(S["rstd"], 1)
                        if layer == 4:
                            break
                        heads = H if layer == 0 else 1
                        wait("f2_range", layer + 1)
                        nc.gpsimd.partition_all_reduce(f2g[:, 0:2 * heads], f2r[:, 0:2 * heads], P, RMAX)\
                            .then_inc(S["f2_gmax"], 1)
                        wait("f2_gmax", layer + 1)
                        rows_at = GEN[layer] + NTR[layer] + NT
                        for h in range(heads):
                            wait("gen_free", rows_at + 2 * (h // 4) + 2)
                            if h >= 2:
                                wait("mplus", h - 1)
                            q = 32 * (h % 4)
                            nc.gpsimd.partition_broadcast(Fb[:, h % 2, :], rows[q:q + 1, h // 4, :])\
                                .then_inc(S["bcast"], 1)
                            wait("bcast", (0 if layer == 0 else 7 + layer) + h + 1)
            for k in range(2):
                pool.wait_ge(t_dve, 2 + 3 * k)
                nc.gpsimd.tensor_tensor(sc[:, 2 + 8 * k:3 + 8 * k], sc[:, 1 + 8 * k:2 + 8 * k], mhalf[:, 0:1],
                                        ALU.pow).then_inc(t_pool, 1)

        @block.scalar
        def _(act):
            def convert(t, par, landed):
                act.wait_ge(adj_land[t % 2], landed)
                nc.scalar.activation(A[:, par, t, :], adj_in[:, t % 2, :], ACT.Copy,
                                     accum_out=deg[:, par, t:t + 1]).then_inc(S["adj_conv"], 1)

            def keep_transposed(u, par):
                nc.scalar.activation(AT[:, par, u, :], tps[:, :], ACT.Copy,
                                     accum_out=cnt[:, par, u:u + 1], saturate=False).then_inc(S["at_ready"], 1)

            for t in range(NT):
                convert(t, 0, 16 * (t // 2 + 1))
            for u in range(NT):
                act.wait_ge(S["at_full"], u + 1)
                keep_transposed(u, 0)
            act.wait_ge(w_pe, 1)
            nc.scalar.activation(WX3[:, 0:F], gen[:, 0, 0:F], ACT.Copy).then_inc(w_act, 1)

            with act.Fori(0, PAIRS) as pair:
                for half in range(2):
                    def wait(name, k):
                        act.wait_ge(S[name], upto(pair, half, name, k))

                    use = [0]

                    def drain(dst, cols_, accum=None, scale=1.0):
                        k = use[0]
                        use[0] += 1
                        wait("gen_full", k + 1)
                        parts = dst.shape[0]
                        if accum is not None:
                            nc.scalar.activation(dst, gen[0:parts, k % 2, 0:cols_], ACT.Copy, scale=scale,
                                                 accum_out=accum).then_inc(S["gen_free"], 1)
                        else:
                            nc.scalar.activation(dst, gen[0:parts, k % 2, 0:cols_], ACT.Copy, scale=scale)\
                                .then_inc(S["gen_free"], 1)

                    def prepare(point):
                        par = 1 - half
                        if point < NT:
                            t = point
                            convert(t, par, pair * 128 + (half * 64 + 64 + 16 * (t // 2 + 1)))
                        else:
                            u = point - NT
                            wait("at_full", NT + u + 1)
                            alone(act, "act")
                            keep_transposed(u, par)

                    for layer in range(5):
                        heads = H if layer == 0 else 1
                        if layer in LN:
                            src = xin if layer == 0 else xw
                            wait("nmr", LN[layer] + 1)
                            for t in range(NT):
                                last = nc.scalar.activation(H0[:, t, :], src[:, t, :], ACT.Relu,
                                                            bias=nmr[:, t:t + 1], scale=rstd[:, t:t + 1])
                                if t % 4 == 3:
                                    last.then_inc(S["h_ready"], 1)
                            for f in range(2):
                                drain(hT[:, f * HALF:(f + 1) * HALF], HALF, csum[:, f:f + 1])
                        else:
                            for k in range(2):
                                for f in range(2):
                                    drain(xcT[:, k, f * HALF:(f + 1) * HALF], HALF, csum[:, 2 * k + f:2 * k + f + 1])
                        if layer == 4:
                            break
                        for t in range(NT):
                            drain((Hn0 if layer == 0 else Hn1)[:, t, :], C0 if layer == 0 else C1)
                        for g in range(2 if layer == 0 else 1):
                            for f in range(2):
                                drain(rows[0:(P if layer == 0 else 1), g, f * HALF:(f + 1) * HALF], HALF)
                        if layer < 3:
                            drain(meanb[:, 0:HD if layer == 0 else F], HD if layer == 0 else F)
                        n = NT * heads
                        wait("args", layer + 1)
                        nc.scalar.activation(fac[:, :, 0:n], args[:, :, 0:n], ACT.Exp).then_inc(S["exps"], 1)
                        Vt = thin_v(layer)
                        Ft = thin_f(layer)
                        wait("v_full", layer + 1)
                        nc.scalar.activation(Vt[:, :, 0, :], Ft, ACT.Copy).then_inc(S["v_hi"], 1)
                        wait("v_rest", layer + 1)
                        nc.scalar.activation(Vt[:, :, 1, :], Ft, ACT.Copy).then_inc(S["v_mid"], 1)

                        def compare(h):
                            first = 0 if layer == 0 else 7 + layer
                            wait("bcast", first + h + 1)
                            if h >= 2:
                                wait("m_used", h - 1)
                            alone(act, "act")
                            for t in range(DVE_CMP, NT):
                                last = nc.scalar.activation(
                                    M[:, h % 2, t, :].bitcast(U8), Fb[:, h % 2, :], ACT.Relu,
                                    bias=bigf2[:, t * heads + h:t * heads + h + 1], scale=STEP_GAIN)
                            last.then_inc(S["act_cmp"], 1)

                        if layer == 0:
                            compare(0)
                            compare(1)
                            for t in range(NT):
                                wait("slot_full", t + 1)
                                nc.scalar.activation(D0[:, t, :, :].rearrange("p h c -> p (h c)"),
                                                     mps[:, t % 4, 0:H * E], ACT.Copy).then_inc(S["act_slot"], 1)
                            for h in range(H):
                                for f in range(2):
                                    k = NT + 2 * h + f
                                    wait("slot_full", k + 1)
                                    nc.scalar.activation(
                                        Vf0[:, 4 * f:4 * f + 4, h, :],
                                        mps[:, k % 4, 0:4 * 2 * E].rearrange("p (t c) -> p t c", t=4),
                                        ACT.Copy).then_inc(S["act_slot"], 1)
                                if h + 2 < H:
                                    compare(h + 2)
                                prepare(h)
                        else:
                            compare(0)
                            for t in range(NT):
                                k = SLOT[layer] + t
                                wait("slot_full", k + 1)
                                if t >= 2:
                                    wait("dve_slot", k - 24 - 1)
                                nc.scalar.activation(Tm[:, t % 2, :], mps[:, k % 4, 0:E1], ACT.Copy,
                                                     scale=fac[:, 0, t:t + 1]).then_inc(S["act_slot"], 1)
                            for u in {1: (8, 9, 10), 2: (11, 12, 13), 3: (14, 15)}[layer]:
                                prepare(u)
                        if layer < 3:
                            wait("mneg", layer + 1)
                            src = Dn[:, 0:NT * (HD if layer == 0 else F)]
                            nc.scalar.activation(src, src, ACT.Exp).then_inc(S["eexp"], 1)

                    for f in range(2):
                        drain(Vf[:, f * HALF:(f + 1) * HALF], HALF)
                    wait("gen_free", use[0])
                    nc.scalar.activation(V3[:, :, 0, :], Vf3, ACT.Copy).then_inc(S["v_hi"], 1)
                    wait("v_rest", 5)
                    nc.scalar.activation(V3[:, :, 1, :], Vf3, ACT.Copy).then_inc(S["v_mid"], 1)
                    wait("v_full", 5)
                    nc.scalar.activation(V3[:, :, 0, :], Vf3, ACT.Copy).then_inc(S["v_hi"], 1)
                    wait("v_rest", 6)
                    nc.scalar.activation(V3[:, :, 1, :], Vf3, ACT.Copy).then_inc(S["v_mid"], 1)
                    drain(q3[:, :, :].rearrange("p t q -> p (t q)"), NT * 3)
                    for f in range(2):
                        drain(GT[:, bass.ds(pair * (2 * N) + (half * N + f * HALF), HALF)], HALF)
                    assert use[0] == PER["gen_free"]
                    wait("dve_done", 1)
                    wait("pe_done", 1)
            act.wait_ge(t_pe, 1)
            nc.scalar.activation(qT[:, :], sps[0:B * NT, 0:P], ACT.Copy).then_inc(t_act, 1)
            act.wait_ge(t_pe, 2)
            nc.scalar.activation(tK2[0:1, :], gen[0:1, 0, 0:F], ACT.Copy).then_inc(t_act, 1)
            for g in range(B * N // 512):
                act.wait_ge(t_gf, g + 1)
                nc.scalar.activation(GT[:, g * 512:(g + 1) * 512], mps[:, g % 4, :], ACT.Identity,
                                     bias=cols[:, 2:3]).then_inc(t_ge, 1)
            act.wait_ge(t_dve, 6)
            for g in range(B * N // 512):
                nc.scalar.activation(GT[:, g * 512:(g + 1) * 512], GT[:, g * 512:(g + 1) * 512], ACT.Identity,
                                     bias=sc[:, 12:13], scale=sc[:, 11:12]).then_inc(t_act, 1)

        @block.vector
        def _(dve):
            dve.wait_ge(w_land, 16 * LOADS)
            dve.wait_ge(w_pool, 4)
            done = [0]

            def setup(ins):
                done[0] += 1
                ins.then_inc(w_dve, 1)
                dve.wait_ge(w_dve, done[0])

            setup(nc.vector.tensor_copy(identb[:, :], ident[:, :]))
            setup(nc.vector.memset(WR0[:, :, :], 0.0))
            setup(nc.vector.memset(bnacc[:, :], 0.0))
            prod = Dn[:, 0:HD].rearrange("p (h d) -> p h d", h=H)
            a1b = Fb[:, 0, 0:2 * HD].rearrange("p (h s d) -> p h s d", h=H, s=2)
            for s in range(2):
                setup(nc.vector.tensor_tensor(prod, WX0[:, 0:HD].rearrange("f (h d) -> f h d", h=H),
                                              a1b[:, :, s, :], ALU.mult))
                setup(nc.vector.tensor_reduce(WX0[:, HD + s * H:HD + (s + 1) * H], prod, AX_X, ALU.add))
            for g in range(2):
                setup(nc.vector.tensor_copy(WR0[:, g, :].rearrange("p (q c) -> p q c", q=4)[:, :, 0],
                                            WX0[:, HD + 4 * g:HD + 4 * g + 4]))
            dve.wait_ge(w_act, 1)
            for W, avec in ((WX1[:, 0, :], Fb[:, 1, 0:2 * F]), (WX1[:, 1, :], Fb[:, 1, 0:2 * F]),
                            (WX2[:, :], Fb[:, 1, 2 * F:4 * F]), (WX3[:, :], Fb[:, 0, 2 * HD:2 * HD + 2 * F])):
                for s in range(2):
                    setup(nc.vector.tensor_tensor(Dn[:, 0:F], W[:, 0:F], avec[:, s * F:(s + 1) * F], ALU.mult))
                    setup(nc.vector.tensor_reduce(W[:, F + s:F + s + 1], Dn[:, 0:F], AX_X, ALU.add))

            with dve.Fori(0, PAIRS) as pair:
                for half in range(2):
                    def wait(name, k):
                        dve.wait_ge(S[name], upto(pair, half, name, k))

                    steps = [0]

                    def go(ins):
                        steps[0] += 1
                        ins.then_inc(dve_chain, 1)

                    def sync():
                        dve.wait_ge(dve_chain, pair * (2 * DVE_STEPS) + (half * DVE_STEPS + steps[0]))

                    def link(ins):
                        go(ins)
                        sync()

                    def parts(Vt, Ft, k):
                        wait("v_hi", k)
                        link(nc.vector.tensor_tensor(Ft, Ft, Vt[:, :, 0, :], ALU.subtract))
                        signal("v_rest")
                        wait("v_mid", k)
                        link(nc.vector.tensor_tensor(Vt[:, :, 2, :], Ft, Vt[:, :, 1, :], ALU.subtract))
                        signal("v_ready")

                    def signal(name):
                        dve.sem_inc(S[name], 1)

                    wait("at_ready", NT)
                    link(nc.vector.tensor_scalar(emp[:, :], deg[:, half, :], 0.0, None, ALU.is_equal))
                    link(nc.vector.tensor_scalar(rcr[:, :], cnt[:, half, :], 1.0, None, ALU.max))
                    link(nc.vector.reciprocal(rc[:, :], rcr[:, :]))
                    link(nc.vector.tensor_copy(rc3[:, :, 0], rc[:, :]))
                    link(nc.vector.tensor_tensor(rcr[:, :], rc[:, :], rc3[:, :, 0], ALU.subtract))
                    link(nc.vector.tensor_copy(rc3[:, :, 1], rcr[:, :]))
                    link(nc.vector.tensor_tensor(rc3[:, :, 2], rcr[:, :], rc3[:, :, 1], ALU.subtract))
                    dve.wait_ge(x_land, pair * 32 + (half * 16 + 16))

                    for layer in range(5):
                        heads = H if layer == 0 else 1
                        n = NT * heads
                        if layer in LN:
                            src = xin if layer == 0 else xw
                            for t in range(NT):
                                go(nc.vector.bn_stats(st6[:, t, :], src[:, t, :]))
                            sync()
                            alone(dve, "dve")
                            for t in range(NT):
                                go(nc.vector.bn_aggr(mv[:, t, :], st6[:, t, :]))
                            sync()
                            link(nc.vector.tensor_scalar(ve[:, :], mv[:, :, 1], LN_EPS, None, ALU.add))
                            signal("ln_var")
                            wait("rstd", LN[layer] + 1)
                            link(nc.vector.scalar_tensor_tensor(nmr[:, :], mv[:, :, 0], -1.0, rstd[:, :],
                                                                ALU.mult, ALU.mult))
                            signal("nmr")
                        if layer == 4:
                            break
                        if layer < 3:
                            wait("gen_free", GEN[layer] + NTR[layer])
                            for k in range(NTR[layer] // 2):
                                link(nc.vector.tensor_tensor(csum[:, 2 * k:2 * k + 1], csum[:, 2 * k:2 * k + 1],
                                                             csum[:, 2 * k + 1:2 * k + 2], ALU.add))
                                link(nc.vector.tensor_scalar(mean_lhs[:, k, :], ones[:, :], csum[:, 2 * k:2 * k + 1],
                                                             1.0 / N, ALU.mult, ALU.mult))
                            signal("mean_lhs")
                        Hv = Hn0 if layer == 0 else Hn1
                        c = HD if layer == 0 else F
                        f1 = Hv[:, :, c:c + heads]
                        f2 = Hv[:, :, c + heads:c + 2 * heads]
                        wait("gen_free", GEN[layer] + NTR[layer] + NT)
                        f2_ht = f2.rearrange("p t h -> p h t")
                        link(nc.vector.tensor_reduce(f2r[:, 0:heads], f2_ht, AX_X, ALU.max))
                        link(nc.vector.tensor_reduce(f2r[:, heads:2 * heads], f2_ht, AX_X, ALU.min))
                        link(nc.vector.tensor_scalar(f2r[:, heads:2 * heads], f2r[:, heads:2 * heads], -1.0, None,
                                                     ALU.mult))
                        signal("f2_range")
                        v3 = lambda ap: ap.rearrange("p (t h) -> p t h", h=heads)
                        link(nc.vector.tensor_scalar(v3(nf2[:, 0:n]), f2, -1.0, None, ALU.mult))
                        link(nc.vector.tensor_scalar(v3(bigf2[:, 0:n]), f2, STEP_GAIN, None, ALU.mult))
                        wait("f2_gmax", layer + 1)
                        link(nc.vector.tensor_tensor(Cb[:, 0:heads], f2g[:, 0:heads], f2g[:, heads:2 * heads],
                                                     ALU.subtract))
                        link(nc.vector.tensor_scalar(Cb[:, 0:heads], Cb[:, 0:heads], 0.5, None, ALU.mult))
                        Cv = Cb[:, 0:heads].rearrange("p (o h) -> p o h", o=1).to_broadcast([P, NT, heads])
                        link(nc.vector.tensor_tensor(v3(sarg[:, 0:n]), f1, Cv, ALU.add))
                        link(nc.vector.tensor_tensor(v3(args[:, 2, 0:n]), f2, Cv, ALU.subtract))
                        link(nc.vector.tensor_scalar(args[:, 0, 0:n], sarg[:, 0:n], 1.0 - SLOPE, 0.0,
                                                     ALU.mult, ALU.min))
                        link(nc.vector.tensor_scalar(args[:, 1, 0:n], sarg[:, 0:n], SLOPE - 1.0, 0.0,
                                                     ALU.mult, ALU.min))
                        link(nc.vector.tensor_scalar(args[:, 3, 0:n], args[:, 2, 0:n], SLOPE, None, ALU.mult))
                        signal("args")
                        wait("exps", layer + 1)
                        w = D if layer == 0 else F
                        for s in range(2):
                            o = s * (w + 1)
                            if layer == 0:
                                dst = Vf0[:, :, :, o:o + w]
                                val = Hn0[:, :, 0:HD].rearrange("p t (h d) -> p t h d", h=H)
                                cf = fac[:, 2 + s, 0:n].rearrange("p (t h o) -> p t h o", h=H, o=1)\
                                    .to_broadcast([P, NT, H, D])
                                one = Vf0[:, :, :, o + w]
                                cv = fac[:, 2 + s, 0:n].rearrange("p (t h) -> p t h", h=H)
                            else:
                                dst = Vf1[:, :, o:o + w]
                                val = Hn1[:, :, 0:F]
                                cf = fac[:, 2 + s, 0:n].rearrange("p (t o) -> p t o", o=1).to_broadcast([P, NT, F])
                                one = Vf1[:, :, o + w]
                                cv = fac[:, 2 + s, 0:n]
                            go(nc.vector.tensor_tensor(dst, val, cf, ALU.mult))
                            go(nc.vector.tensor_copy(one, cv))
                        sync()
                        signal("v_full")

                        def select(h):
                            first = 0 if layer == 0 else 7 + layer
                            wait("bcast", first + h + 1)
                            if h >= 2:
                                wait("m_used", h - 1)
                            alone(dve, "dve")
                            for t in range(DVE_CMP):
                                k = t * heads + h
                                go(nc.vector.tensor_scalar(M[:, h % 2, t, :], Fb[:, h % 2, :], nf2[:, k:k + 1], None,
                                                           ALU.is_ge, saturate=False))
                            sync()
                            wait("act_cmp", first + h + 1)
                            for f in range(2):
                                m = M[:, h % 2, 4 * f:4 * f + 4, :].bitcast(U32)
                                a = AT[:, half, 4 * f:4 * f + 4, :].bitcast(U32)
                                go(nc.vector.tensor_tensor(m, m, a, ALU.bitwise_and))
                            sync()
                            signal("mplus")

                        parts(thin_v(layer), thin_f(layer), layer + 1)
                        for h in range(heads):
                            select(h)
                        if layer == 0:
                            wait("act_slot", 3 * NT)
                            num, Ub, Ud = thin(D0), thin(Vf0)[:, :, 0:E], thin(Vf0)[:, :, E:2 * E]
                            ca = fac[:, 0, 0:n].rearrange("p (n o) -> p n o", o=1).to_broadcast([P, n, E])
                            cc = fac[:, 1, 0:n].rearrange("p (n o) -> p n o", o=1).to_broadcast([P, n, E])
                            link(nc.vector.tensor_tensor(num, num, Ud, ALU.subtract))
                            go(nc.vector.tensor_tensor(Ub, Ub, ca, ALU.mult))
                            link(nc.vector.tensor_tensor(num, num, cc, ALU.mult))
                            link(nc.vector.tensor_tensor(num, num, Ub, ALU.add))
                            den = D0[:, :, :, D]
                            ev = emp[:, :].rearrange("p (t o) -> p t o", o=1).to_broadcast([P, NT, H])
                            link(nc.vector.tensor_tensor(v3(rden[:, 0:n]), den, ev, ALU.add))
                            link(nc.vector.reciprocal(rden[:, 0:n], rden[:, 0:n]))
                            rv = rden[:, 0:n].rearrange("p (t h o) -> p t h o", h=H, o=1).to_broadcast([P, NT, H, D])
                            link(nc.vector.tensor_tensor(xc.rearrange("p t (h d) -> p t h d", h=H),
                                                         D0[:, :, :, 0:D], rv, ALU.mult))
                            o_all, width = xc, HD
                        else:
                            for f in range(2):
                                m = M[:, 0, 4 * f:4 * f + 4, :].bitcast(U32)
                                mm = M[:, 1, 4 * f:4 * f + 4, :].bitcast(U32)
                                a = AT[:, half, 4 * f:4 * f + 4, :].bitcast(U32)
                                go(nc.vector.tensor_tensor(mm, m, a, ALU.bitwise_xor))
                            sync()
                            signal("mminus")
                            for t in range(NT):
                                k = SLOT[layer] + t
                                wait("act_slot", k + 1)
                                nc.vector.scalar_tensor_tensor(D1[:, t, :], mps[:, k % 4, E1:2 * E1],
                                                               fac[:, 1, t:t + 1], Tm[:, t % 2, :],
                                                               ALU.mult, ALU.add).then_inc(S["dve_slot"], 1)
                            wait("dve_slot", SLOT[layer] - 24 + NT)
                            link(nc.vector.tensor_tensor(rden[:, 0:NT], D1[:, :, F], emp[:, :], ALU.add))
                            link(nc.vector.reciprocal(rden[:, 0:NT], rden[:, 0:NT]))
                            rv = rden[:, 0:NT].rearrange("p (t o) -> p t o", o=1).to_broadcast([P, NT, F])
                            o_all, width = Vf3, F
                            link(nc.vector.tensor_tensor(o_all, D1[:, :, 0:F], rv, ALU.mult))
                        if layer < 3:
                            for t in range(NT):
                                go(nc.vector.scalar_tensor_tensor(o_all[:, t, :], meanb[:, 0:width], emp[:, t:t + 1],
                                                                  o_all[:, t, :], ALU.mult, ALU.add))
                            sync()
                            ex = Dn[:, 0:NT * width].rearrange("p (t c) -> p t c", t=NT)
                            link(nc.vector.tensor_scalar(ex, o_all, 0.0, None, ALU.min))
                            signal("mneg")
                            wait("eexp", layer + 1)
                            link(nc.vector.scalar_tensor_tensor(o_all, ex, -1.0, o_all, ALU.add, ALU.max))
                        if layer == 0:
                            signal("xc_ready")
                        elif layer == 1:
                            link(nc.vector.tensor_tensor(xw[:, :, :], xin[:, :, :], H0[:, :, :], ALU.add))
                            signal("x1_ready")
                            link(nc.vector.tensor_tensor(xw[:, :, :], xw[:, :, :], Vf3, ALU.add))
                        else:
                            link(nc.vector.tensor_tensor(xw[:, :, :], xw[:, :, :], Vf3, ALU.add))
                            if layer == 3:
                                signal("x3_ready")

                    parts(V3, Vf3, 5)
                    for t in range(NT):
                        k = SLOT[4] + t
                        wait("slot_full", k + 1)
                        nc.vector.scalar_tensor_tensor(D3[:, t, :], mps[:, k % 4, 0:F], rc[:, t:t + 1], b1b[:, :],
                                                       ALU.mult, ALU.add).then_inc(S["dve_slot"], 1)
                    wait("dve_slot", 4 * NT)
                    rv = rc[:, :].rearrange("p (t o) -> p t o", o=1).to_broadcast([P, NT, F])
                    go(nc.vector.tensor_tensor(Vf3, D3, rv, ALU.mult))
                    go(nc.vector.tensor_tensor(sq3, D3, D3, ALU.mult))
                    sync()
                    signal("v_full")
                    signal("region")
                    parts(V3, Vf3, 6)
                    wait("stats", 1)
                    link(nc.vector.tensor_tensor(bnacc[:, :], bnacc[:, :], sps[:, 0:2], ALU.add))
                    wait("gen_free", GEN[4] + 5)
                    link(nc.vector.tensor_reduce(Qall[:, bass.ds(pair * (2 * NT) + half * NT, NT)], q3[:, :, :],
                                                 AX_X, ALU.add))
                    signal("dve_done")
                    assert steps[0] == DVE_STEPS, steps[0]
                    wait("gen_free", PER["gen_free"])
                    wait("pe_done", 1)
                    dve.wait_ge(x3_store, pair * 32 + (half * 16 + 16))

            rows_all = B * N
            tick = [0]

            def tlink(ins):
                tick[0] += 1
                ins.then_inc(t_free, 1)
                dve.wait_ge(t_free, tick[0])

            tlink(nc.vector.tensor_scalar(sc[:, 4:6], bnacc[:, :], 1.0 / rows_all, None, ALU.mult))
            tlink(nc.vector.tensor_tensor(sc[:, 6:7], sc[:, 4:5], sc[:, 4:5], ALU.mult))
            tlink(nc.vector.scalar_tensor_tensor(sc[:, 1:2], sc[:, 6:7], -1.0, sc[:, 5:6], ALU.mult, ALU.add))
            tlink(nc.vector.tensor_scalar(sc[:, 1:2], sc[:, 1:2], BN_EPS, None, ALU.add))
            dve.sem_inc(t_dve, 2)
            dve.wait_ge(t_pool, 1)
            tlink(nc.vector.tensor_tensor(sc[:, 7:8], sc[:, 2:3], cols[:, 0:1], ALU.mult))
            tlink(nc.vector.tensor_tensor(sc[:, 6:7], sc[:, 4:5], sc[:, 7:8], ALU.mult))
            tlink(nc.vector.tensor_tensor(sc[:, 8:9], cols[:, 1:2], sc[:, 6:7], ALU.subtract))
            tlink(nc.vector.tensor_scalar(hT[:, 0:F], K2s[:, :], sc[:, 7:8], None, ALU.mult))
            dve.sem_inc(t_dve, 2)
            for g in range(B * N // 512):
                dve.wait_ge(t_ge, g + 1)
                nc.vector.bn_stats(bst[:, g, :], GT[:, g * 512:(g + 1) * 512]).then_inc(t_free, 1)
                tick[0] += 1
            dve.wait_ge(t_free, tick[0])
            tlink(nc.vector.bn_aggr(sc[:, 4:6], bst[:, :, :].rearrange("p g s -> p (g s)")))
            tlink(nc.vector.tensor_scalar(sc[:, 9:10], sc[:, 5:6], BN_EPS, None, ALU.add))
            dve.sem_inc(t_dve, 1)
            dve.wait_ge(t_pool, 2)
            tlink(nc.vector.tensor_tensor(sc[:, 11:12], sc[:, 10:11], cols[:, 3:4], ALU.mult))
            tlink(nc.vector.tensor_tensor(sc[:, 6:7], sc[:, 4:5], sc[:, 11:12], ALU.mult))
            tlink(nc.vector.tensor_tensor(sc[:, 12:13], cols[:, 4:5], sc[:, 6:7], ALU.subtract))
            dve.sem_inc(t_dve, 1)
            X3 = A[:, :, :, :].rearrange("p a t n -> p (a t n)").bitcast(F32).rearrange("p (g c) -> p g c", c=512)
            dve.wait_ge(t_x3, 16)
            for g in range(B * N // 512):
                dve.wait_ge(t_pe, 3 + g)
                nc.vector.tensor_tensor(X3[:, g, :], X3[:, g, :], gen[:, g % 2, :], ALU.add).then_inc(t_out, 1)

        @block.tensor
        def _(pe):
            pe.wait_ge(w_land, 16 * LOADS)
            pe.wait_ge(w_pool, 4)
            nc.tensor.transpose(gen[:, 0, 0:F], H0[:, 0, :], ident[:, :]).then_inc(w_pe, 1)

            def transpose_adjacency(u, par):
                for t in range(NT):
                    last = nc.tensor.transpose(tps[:, t * P:(t + 1) * P], A[:, par, t, u * P:(u + 1) * P],
                                               identb[:, :])
                last.then_inc(S["at_full"], 1)

            pe.wait_ge(w_dve, 1)
            pe.wait_ge(S["adj_conv"], NT)
            for u in range(NT):
                if u:
                    pe.wait_ge(S["at_ready"], u)
                transpose_adjacency(u, 0)
            pe.wait_ge(w_dve, 17)

            with pe.Fori(0, PAIRS) as pair:
                for half in range(2):
                    def wait(name, k):
                        pe.wait_ge(S[name], upto(pair, half, name, k))

                    use = [0]

                    def bank():
                        k = use[0]
                        if k >= 2:
                            wait("gen_free", k - 1)
                        use[0] += 1
                        return gen[:, k % 2, :]

                    def prepare(u):
                        wait("adj_conv", 2 * NT)
                        wait("at_ready", NT + u)
                        transpose_adjacency(u, 1 - half)

                    for layer in range(5):
                        heads = H if layer == 0 else 1
                        assert use[0] == GEN[layer]
                        if layer in LN:
                            for f in range(2):
                                wait("h_ready", 2 * LN[layer] + f + 1)
                                o = bank()
                                for t in range(4):
                                    last = nc.tensor.transpose(o[:, t * P:(t + 1) * P], H0[:, 4 * f + t, :], ident[:, :])
                                last.then_inc(S["gen_full"], 1)
                            chunks = [hT[:, :]]
                        else:
                            wait("xc_ready", 1)
                            for k in range(2):
                                for f in range(2):
                                    o = bank()
                                    for t in range(4):
                                        last = nc.tensor.transpose(o[:, t * P:(t + 1) * P],
                                                                   xc[:, 4 * f + t, k * P:(k + 1) * P], ident[:, :])
                                    last.then_inc(S["gen_full"], 1)
                            chunks = [xcT[:, 0, :], xcT[:, 1, :]]
                        wait("gen_free", GEN[layer] + NTR[layer])
                        if layer == 4:
                            break
                        nk = len(chunks)
                        WX = {0: [WX0[:, :]], 1: [WX1[:, 0, :], WX1[:, 1, :]], 2: [WX2[:, :]], 3: [WX3[:, :]]}[layer]
                        width = C0 if layer == 0 else C1
                        for t in range(NT):
                            o = bank()
                            for k in range(nk):
                                last = nc.tensor.matmul(o[:, 0:width], chunks[k][:, t * P:(t + 1) * P], WX[k],
                                                        start=(k == 0), stop=(k == nk - 1))
                            last.then_inc(S["gen_full"], 1)
                        for g in range(2 if layer == 0 else 1):
                            for f in range(2):
                                o = bank()
                                for k in range(nk):
                                    if layer == 0:
                                        last = nc.tensor.matmul(o, WR0[:, g, :], hT[:, f * HALF:(f + 1) * HALF],
                                                                start=True, stop=True)
                                    else:
                                        last = nc.tensor.matmul(o[0:1, :], WX[k][:, F:F + 1],
                                                                chunks[k][:, f * HALF:(f + 1) * HALF],
                                                                start=(k == 0), stop=(k == nk - 1))
                                last.then_inc(S["gen_full"], 1)
                        if layer < 3:
                            wait("mean_lhs", layer + 1)
                            wv = HD if layer == 0 else F
                            o = bank()
                            for k in range(nk):
                                last = nc.tensor.matmul(o[:, 0:wv], mean_lhs[:, k, :], WX[k][:, 0:wv],
                                                        start=(k == 0), stop=(k == nk - 1))
                            last.then_inc(S["gen_full"], 1)
                        wait("v_ready", layer + 1)
                        if layer == 0:
                            for i in range(NT):
                                if i >= 4:
                                    wait("act_slot", i - 3)
                                alone(pe, "pe")
                                for j in range(NT):
                                    for q in range(3):
                                        last = nc.tensor.matmul(
                                            mps[:, i % 4, 0:H * E], AT[:, half, j, i * P:(i + 1) * P],
                                            V0[:, j, :, q, E:2 * E], start=(j == 0 and q == 0),
                                            stop=(j == NT - 1 and q == 2))
                                last.then_inc(S["slot_full"], 1)
                            for h in range(H):
                                wait("mplus", h + 1)
                                for f in range(2):
                                    k = NT + 2 * h + f
                                    wait("act_slot", k - 3)
                                    alone(pe, "pe")
                                    for i in range(4):
                                        for j in range(NT):
                                            for q in range(3):
                                                last = nc.tensor.matmul(
                                                    mps[:, k % 4, i * 2 * E:(i + 1) * 2 * E],
                                                    M[:, h % 2, j, (4 * f + i) * P:(4 * f + i + 1) * P],
                                                    V0[:, j, h, q, :], start=(j == 0 and q == 0),
                                                    stop=(j == NT - 1 and q == 2))
                                    if f == 0:
                                        last.then_inc(S["slot_full"], 1)
                                last.then_inc(S["slot_full"], 1)
                                wait("slot_full", NT + 2 * h + 2)
                                pe.sem_inc(S["m_used"], 1)
                        else:
                            wait("mplus", 7 + layer + 1)
                            wait("mminus", layer)
                            for i in range(NT):
                                k = SLOT[layer] + i
                                if i >= 4:
                                    wait("dve_slot", k - 24 - 3)
                                alone(pe, "pe")
                                for s in range(2):
                                    for j in range(NT):
                                        for q in range(3):
                                            last = nc.tensor.matmul(
                                                mps[:, k % 4, s * E1:(s + 1) * E1], M[:, s, j, i * P:(i + 1) * P],
                                                V1[:, j, q, s * E1:(s + 1) * E1], start=(j == 0 and q == 0),
                                                stop=(j == NT - 1 and q == 2))
                                last.then_inc(S["slot_full"], 1)
                            wait("slot_full", SLOT[layer] + NT)
                            pe.sem_inc(S["m_used"], 1)
                            for u in {1: (0, 1, 2), 2: (3, 4, 5), 3: (6, 7)}[layer]:
                                prepare(u)

                    for f in range(2):
                        o = bank()
                        for t in range(4):
                            last = nc.tensor.matmul(o[:, t * P:(t + 1) * P], hT[:, (4 * f + t) * P:(4 * f + t + 1) * P],
                                                    K1s[:, :], start=True, stop=True)
                        last.then_inc(S["gen_full"], 1)
                    wait("v_ready", 5)
                    for i in range(NT):
                        k = SLOT[4] + i
                        if i >= 4:
                            wait("dve_slot", k - 24 - 3)
                        for j in range(NT):
                            for q in range(3):
                                last = nc.tensor.matmul(mps[:, k % 4, 0:F], A[:, half, j, i * P:(i + 1) * P],
                                                        V3[:, j, q, :], start=(j == 0 and q == 0),
                                                        stop=(j == NT - 1 and q == 2))
                        last.then_inc(S["slot_full"], 1)
                    wait("region", 1)
                    for s, src in ((0, D3), (1, sq3)):
                        for t in range(NT):
                            last = nc.tensor.matmul(sps[:, s:s + 1], src[:, t, :], ones[:, 0:1],
                                                    start=(t == 0), stop=(t == NT - 1))
                    last.then_inc(S["stats"], 1)
                    o = bank()
                    alone(pe, "pe")
                    for i in range(NT):
                        for j in range(NT):
                            last = nc.tensor.matmul(o[:, 3 * i:3 * i + 3], AT[:, half, j, i * P:(i + 1) * P],
                                                    rc3[:, j, :], start=(j == 0), stop=(j == NT - 1))
                    last.then_inc(S["gen_full"], 1)
                    wait("v_ready", 6)
                    for f in range(2):
                        o = bank()
                        alone(pe, "pe")
                        for j in range(NT):
                            for q in range(3):
                                last = nc.tensor.matmul(o, V3[:, j, q, :], AT[:, half, j, f * HALF:(f + 1) * HALF],
                                                        start=(j == 0 and q == 0), stop=(j == NT - 1 and q == 2))
                        last.then_inc(S["gen_full"], 1)
                    assert use[0] == PER["gen_full"]
                    wait("gen_full", PER["gen_full"])
                    pe.sem_inc(S["pe_done"], 1)
                    wait("gen_free", PER["gen_free"])
                    wait("dve_done", 1)

            nc.tensor.transpose(sps[0:B * NT, 0:P], Qall[:, :], ident[:, :]).then_inc(t_pe, 1)
            pe.wait_ge(t_dve, 4)
            nc.tensor.matmul(gen[0:1, 0, 0:F], sc[:, 8:9], K2s[:, :], start=True, stop=True).then_inc(t_pe, 1)
            pe.wait_ge(t_act, 2)
            pe.wait_ge(t_ld, 32)
            qrow = [M, AT]
            for g in range(B * N // 512):
                if g >= 4:
                    pe.wait_ge(t_ge, g - 3)
                q = qrow[g // 8][0:1, :, :, :].rearrange("o a t n -> o (a t n)").bitcast(F32)
                nc.tensor.matmul(mps[:, g % 4, :], hT[:, 0:F], GT[:, g * 512:(g + 1) * 512], start=True, stop=False)
                nc.tensor.matmul(mps[:, g % 4, :], tK2[0:1, :], q[:, (g % 8) * 512:(g % 8 + 1) * 512],
                                 start=False, stop=True).then_inc(t_gf, 1)
            for g in range(B * N // 512):
                pe.wait_ge(t_act, 3 + g)
                if g >= 2:
                    pe.wait_ge(t_out, g - 1)
                for t in range(4):
                    last = nc.tensor.transpose(gen[:, g % 2, t * P:(t + 1) * P],
                                               GT[:, g * 512 + t * P:g * 512 + (t + 1) * P], ident[:, :])
                last.then_inc(t_pe, 1)


def kernel(x, adj, L0_gnn_W1, L0_gnn_a1, L0_gnn_W2, L0_gnn_a2, L1_gnn_W, L1_gnn_a, L2_gnn_W, L2_gnn_a,
           L3_gnn_kernel_1, L3_gnn_bias_1, L3_gnn_gamma_1, L3_gnn_beta_1,
           L3_gnn_kernel_2, L3_gnn_bias_2, L3_gnn_gamma_2, L3_gnn_beta_2):
    import concourse.bacc as bacc
    import numpy as np
    from concourse.bass_utils import run_bass_kernel_spmd

    names = ["x", "adj", "L0_W1", "L0_a1", "L0_W2", "L0_a2", "L1_W", "L1_a", "L2_W", "L2_a", "L3_K1", "L3_b1",
             "L3_gamma1", "L3_beta1", "L3_K2", "L3_b2", "L3_gamma2", "L3_beta2"]
    given = [x, adj, L0_gnn_W1, L0_gnn_a1, L0_gnn_W2, L0_gnn_a2, L1_gnn_W, L1_gnn_a, L2_gnn_W, L2_gnn_a,
             L3_gnn_kernel_1, L3_gnn_bias_1, L3_gnn_gamma_1, L3_gnn_beta_1,
             L3_gnn_kernel_2, L3_gnn_bias_2, L3_gnn_gamma_2, L3_gnn_beta_2]
    nc = bacc.Bacc("TRN2", target_bir_lowering=False, num_devices=1)
    arrays, aps = {}, []
    for name, a in zip(names, given):
        a = np.ascontiguousarray(a)
        arrays["in_" + name] = a
        aps.append(nc.dram_tensor("in_" + name, a.shape, mybir.dt.from_np(a.dtype), kind="ExternalInput").ap())
    out = nc.dram_tensor("out_0", x.shape, F32, kind="ExternalOutput").ap()
    adjacency_gnn_stack(nc, *aps, out)
    got = run_bass_kernel_spmd(nc, [arrays], core_ids=[0])
    return got.results[0]["out_0"]
```

```python
from contextlib import ExitStack

import concourse.bass as bass
from concourse import mybir

F32 = mybir.dt.float32
BF16 = mybir.dt.bfloat16
FP8 = mybir.dt.float8e4
I32 = mybir.dt.int32
U32 = mybir.dt.uint32
U8 = mybir.dt.uint8
ALU = mybir.AluOpType
ACT = mybir.ActivationFunctionType
AX_X = mybir.AxisListType.X
RMAX = bass.bass_isa.ReduceOp.max

P = 128
SLOPE = 0.2
LN_EPS = 1e-5
BN_EPS = 1e-3
STEP_GAIN = 1e30
LOADS = 16

EARLY = dict(ln_var=1, rstd=1, nmr=1, h_ready=2, res_h=1, gen_full=26, gen_free=26, mean_lhs=2, f2_range=2, f2_gmax=2,
             args=2, exps=2, v_full=4, v_hi=4, v_rest=4, v_mid=4, v_ready=4, bcast=9, act_cmp=10,
             mplus=10, slot_full=32, act_slot=32, mneg=4, eexp=4, xc_ready=2, mminus=2)
LATE = dict(ln_var=3, rstd=3, nmr=3, h_ready=6, gen_full=23, gen_free=23, mean_lhs=1, f2_range=2, f2_gmax=2,
            args=2, exps=2, v_full=5, v_hi=6, v_rest=6, v_mid=6, v_ready=6, bcast=2, act_cmp=4, mplus=4,
            slot_full=24, act_slot=24, mneg=2, eexp=2, mminus=4, x3_ready=1, region=1)
PREP = dict(adj_conv=8, at_full=8, at_ready=8, a8_done=8, deg_ready=1)
CHAIN_FIRST, CHAIN_TURN = 243, 748


class Graph:

    def __init__(self, pair, off):
        self.pair, self.off, self.par = pair, off, off % 2

    def value(self, per, k):
        if isinstance(self.pair, int):
            return (2 * self.pair + self.off) * per + k
        return self.pair * (2 * per) + (self.off * per + k)

    def next(self, n):
        return Graph(self.pair, self.off + n)


ORDER = """
A cut2 0 0, L ln 2 0, L ln 2 1, A mask 0, L lin 2, A val 0 1, A sel 0 0, A cut1 0 1, A mask 1, A mask 2,
L proj 2, L rows 2, L rng 2, L val 2 0, L val 2 1, A cut2 0 1, L cut1 2 0, A mask 3, A mask 4, A sel 0 1,
A mask 5, L sel 2 0, C conv 0, A mask 6, A mask 7, L cut1 2 1, A head 0 0, A head 0 1, L cut2 2 0, L cut2 2 1,
A sel 0 2, A head 1 0, A head 1 1, A sel 0 3, L slot 2 0, L slot 2 1, L slot 2 2, L sel 2 1, L slot 2 3,
A head 2 0, L mean 2, A head 2 1, L slot 2 4, L post1 2 0, L post2 2 0, A sel 0 4, C conv 1, A head 3 0,
A sel 0 5, A head 3 1, L slot 2 5, L slot 2 6, L post3 2 0, C conv 2, L slot 2 7, L post1 2 1, L post2 2 1,
L ln 3 0, A head 4 0, C conv 3, A head 4 1, L post3 2 1, L ln 3 1, A head 5 0, L lin 3, A comb1 0, A sel 0 6,
A head 5 1, A sel 0 7, L proj 3, L rows 3, L rng 3, L val 3 0, L val 3 1, C conv 4, C conv 5, L cut1 3 0,
L sel 3 0, L cut1 3 1, A head 6 0, A head 6 1, L cut2 3 0, L cut2 3 1, A comb2 0, A head 7 0, A head 7 1,
A comb1 1, L slot 3 0, L slot 3 1, L sel 3 1, A comb2 1, L slot 3 2, A comb3 0, L slot 3 3, L post1 3 0,
L slot 3 4, L post2 3 0, L post3 3 0, L slot 3 5, L slot 3 6, A comb3 1, A lin 1 0, L ln 4 0, L slot 3 7,
A lin 1 1, L post1 3 1, A proj 1, L post2 3 1, L post3 3 1, L ln 4 1, A rows 1, L lin 4, A rng 1, A val 1 0,
C ln 0 0, L gproj, L cut1 4 0, L cut2 4 0, A mean 1, A val 1 1, A cut1 1 0, A cut1 1 1, L gagg 0, A sel 1 0,
L gagg 1, L gagg 2, A cut2 1 0, L gagg 3, L gagg 4, A cut2 1 1, C conv 6, L gagg 5, A sel 1 1, L gagg 6,
A slot 1 0, L gagg 7, A slot 1 1, L greg, L cut1 4 1, A slot 1 2, A slot 1 3, L cut2 4 1, L gstat, A slot 1 4,
A post1 1 0, A post2 1 0, A slot 1 5, A slot 1 6, C ln 0 1, A post3 1 0, C conv 7, L gq, A slot 1 7, L gout,
A post1 1 1, A post2 1 1, C a8 0, C a8 1, C tr 0, C a8 2, A post3 1 1, C tr 1, C lin 0, C a8 3, C tr 2,
C proj 0, C tr 3, C rows 0, C rng 0, C tr 4, C a8 4, C val 0 0, C tr 5, C a8 5, C cut1 0 0, L gend, C a8 6,
C tr 6, C mean 0, C tr 7, C a8 7, C degrees
"""


def order(classes):
    steps = []
    for step in ORDER.split(","):
        of, name, *args = step.split()
        if of in classes:
            steps.append((name, "LAC".index(of), *map(int, args)))
    return steps


class Stream:
    pass


def adjacency_gnn_stack(nc, x, adj, W1, a1, W2, a2, gW, ga, lW, la, K1, b1, gam1, bet1, K2, b2, gam2, bet2, out):
    B, N, F = x.shape
    H, _, D = W1.shape
    NT = N // P
    HD = H * D
    E = D + 1
    E1 = F + 1
    C0 = HD + 2 * H
    C1 = F + 2
    HALF = N // 2
    HT = NT // 2
    DVE_CMP = 5
    TURNS = (B - 2) // 2
    assert F == P and N == 1024 and B % 2 == 0 and H == 8

    with ExitStack() as ctx:
        def sb(name, shape, dt):
            return ctx.enter_context(nc.sbuf_tensor(name, shape, dt))

        def pb(name, shape, dt):
            return ctx.enter_context(nc.psum_tensor(name, shape, dt))

        def sem(name):
            return ctx.enter_context(nc.semaphore(name))

        ADJ = sb("ADJ", [P, 6 * NT * N], FP8)
        A16 = ADJ[:, 0:2 * NT * N].bitcast(BF16).rearrange("p (t n) -> p t n", t=NT)
        A8 = ADJ[:, 2 * NT * N:4 * NT * N].rearrange("p (g t n) -> p g t n", g=2, t=NT)
        AT = ADJ[:, 4 * NT * N:6 * NT * N].rearrange("p (g t n) -> p g t n", g=2, t=NT)
        adj_in = sb("adj_in", [P, 2, N], I32)
        xres = sb("xres", [P, 2, NT, F], F32)
        WX0 = sb("WX0", [P, C0], F32)
        WR0 = sb("WR0", [P, 2, P], F32)
        WX1 = sb("WX1", [P, 2, C1], F32)
        WX2 = sb("WX2", [P, C1], F32)
        WX3 = sb("WX3", [P, C1], F32)
        K1s = sb("K1s", [P, F], F32)
        K2s = sb("K2s", [P, F], F32)
        b1b = sb("b1b", [P, F], F32)
        cols = sb("cols", [P, 8], F32)
        ident = sb("ident", [P, P], F32)
        identb = sb("identb", [P, P], BF16)
        ones = sb("ones", [P, P], F32)
        mhalf = sb("mhalf", [P, NT], F32)
        deg = sb("deg", [P, NT], F32)
        cnt = sb("cnt", [P, NT], F32)
        emp = sb("emp", [P, 2, NT], F32)
        rc = sb("rc", [P, 2, NT], F32)
        rcr = sb("rcr", [P, NT], F32)
        rc3 = sb("rc3", [P, 2, NT, 3], BF16)
        q3 = sb("q3", [P, NT, 3], F32)
        Qall = sb("Qall", [P, B * NT], F32)
        bn_g = sb("bn_g", [P, 2], F32)
        bnacc = sb("bnacc", [P, 2], F32)
        sc = sb("sc", [P, 16], F32)
        tK2 = sb("tK2", [3, F], F32)
        tK2p = sb("tK2p", [3, 3, F], BF16)
        bst = sb("bst", [P, B * N // 512, 6], F32)
        x3_dram = nc.dram_tensor("x3_dram", (B * N, F), F32).ap()
        gt_dram = nc.dram_tensor("gt_dram", (P, B * N), F32).ap()

        def stream(name, per, heads, v_floats, gen_banks):
            st = Stream()
            st.per, st.name = per, name
            st.S = {k: sem(f"{name}_{k}") for k in per}
            n = NT * heads
            st.vf = sb(name + "_vf", [P, v_floats + (v_floats * 3 + 1) // 2], F32)
            st.Vf = st.vf[:, 0:v_floats]
            st.V = st.vf[:, v_floats:].bitcast(BF16)
            st.Dn = sb(name + "_dn", [P, NT * H * E if heads > 1 else N], F32)
            st.hT = st.Dn[:, 0:N]
            st.Hn = sb(name + "_hn", [P, NT * (C0 if heads > 1 else C1)], F32)
            st.Fb = (sb(name + "_fb", [P, 2, N], F32) if heads > 1
                     else st.Dn[:, 0:N].rearrange("p (g n) -> p g n", g=1))
            st.M = sb(name + "_m", [P, 2 if heads > 1 else 1, NT, N], FP8)
            st.meanb = sb(name + "_meanb", [P, HD if heads > 1 else F], F32)
            st.mean_lhs = sb(name + "_mlhs", [P, 2 if heads > 1 else 1, P], F32)
            st.csum = sb(name + "_csum", [P, 4], F32)
            st.st6 = sb(name + "_st6", [P, NT, 6], F32)
            st.mv = sb(name + "_mv", [P, NT, 2], F32)
            st.ve = sb(name + "_ve", [P, NT], F32)
            st.rstd = sb(name + "_rstd", [P, NT], F32)
            st.nmr = sb(name + "_nmr", [P, NT], F32)
            st.f2r = sb(name + "_f2r", [P, 2 * heads], F32)
            st.f2g = sb(name + "_f2g", [P, 2 * heads], F32)
            st.Cb = sb(name + "_cb", [P, heads], F32)
            st.nf2 = sb(name + "_nf2", [P, n], F32)
            st.bigf2 = sb(name + "_bigf2", [P, n], F32)
            st.sarg = sb(name + "_sarg", [P, n], F32)
            st.args = sb(name + "_args", [P, 4, n], F32)
            st.fac = sb(name + "_fac", [P, 4, n], F32)
            st.rden = sb(name + "_rden", [P, n], F32)
            st.gen = pb(name + "_gen", [P, gen_banks, 512], F32)
            st.mps = pb(name + "_mps", [P, 2, 512], F32)
            st.banks = gen_banks
            return st

        early = stream("early", EARLY, H, NT * H * 2 * E, 2)
        late = stream("late", LATE, 1, NT * 2 * E1, 1)
        prep = Stream()
        prep.per, prep.S = PREP, {k: sem("prep_" + k) for k in PREP}
        early.rows = sb("early_rows", [P, 2, N], F32)
        late.rows = late.Vf[:, N:2 * N].rearrange("p (g n) -> p g n", g=1)
        early.Hin = early.Dn[:, N:2 * N].rearrange("p (t f) -> p t f", t=NT)
        late.Hin = late.Vf[:, 0:N].rearrange("p (t f) -> p t f", t=NT)
        tps = pb("tps", [P, N], BF16)

        dve_chain = sem("dve_chain")
        adj_land = [sem("adj_land0"), sem("adj_land1")]
        x_land = [sem("x_land0"), sem("x_land1")]
        x3_store, gt_store, w_land = sem("x3_store"), sem("gt_store"), sem("w_land")
        w_pool, w_dve, w_pe, w_act = sem("w_pool"), sem("w_dve"), sem("w_pe"), sem("w_act")
        t_chain, t_var, t_rstd, t_scale, t_qT, t_qp, t_tK2, t_tp = (sem("t_chain"), sem("t_var"), sem("t_rstd"),
                                                        sem("t_scale"), sem("t_qT"), sem("t_qp"), sem("t_tK2"), sem("t_tp"))
        t_x3, t_q, t_out, t_store = sem("t_x3"), sem("t_q"), sem("t_out"), sem("t_store")
        t_gt = [sem(f"t_gt{n}") for n in range(4)]
        t_peq, t_petk, t_full, t_kept, t_norm, t_back = (sem("t_peq"), sem("t_petk"), sem("t_full"), sem("t_kept"),
                                                         sem("t_norm"), sem("t_back"))
        passed = {e: sem("passed_" + e) for e in ("pe", "act", "dve", "pool", "sp")}

        for st in (early, late):
            st.V1 = st.V[:, 0:NT * 3 * 2 * E1].rearrange("p (t q c) -> p t q c", t=NT, q=3)
            st.Vf1 = st.Vf[:, 0:NT * 2 * E1].rearrange("p (t c) -> p t c", t=NT)
            st.Hn1 = st.Hn[:, 0:NT * C1].rearrange("p (t c) -> p t c", t=NT)
            st.O1 = st.Dn[:, 0:NT * F].rearrange("p (t c) -> p t c", t=NT)
            st.ex1 = st.Vf[:, 0:NT * F].rearrange("p (t c) -> p t c", t=NT)
        V0 = early.V[:, 0:NT * H * 3 * 2 * E].rearrange("p (t h q c) -> p t h q c", t=NT, h=H, q=3)
        Vf0 = early.Vf.rearrange("p (t h c) -> p t h c", t=NT, h=H)
        D0 = early.Dn[:, :].rearrange("p (t h c) -> p t h c", t=NT, h=H)
        Hn0 = early.Hn[:, :].rearrange("p (t c) -> p t c", t=NT)
        xc = early.Hn[:, 0:NT * HD].rearrange("p (t c) -> p t c", t=NT)
        ex0 = early.Dn[:, :].rearrange("p (t k c) -> p t k c", t=NT, k=2)[:, :, :, 0:P]
        xcT = early.rows
        V3 = late.V[:, 0:NT * 3 * F].rearrange("p (t q c) -> p t q c", t=NT, q=3)
        Vf3 = late.ex1
        region = late.O1
        square = late.Hn[:, 0:N].rearrange("p (t c) -> p t c", t=NT)
        GTs = late.Hn[:, 0:N]

        def parts_of(layer):
            if layer == 0:
                return (early.V[:, 0:NT * H * 3 * 2 * E].rearrange("p (n q c) -> p n q c", q=3, c=2 * E),
                        early.Vf.rearrange("p (n c) -> p n c", c=2 * E))
            if layer == 4:
                return V3, Vf3
            st = late if layer > 1 else early
            return st.V1, st.Vf1

        def of(layer):
            return early if layer < 2 else late

        def halves(st, f):
            m = st.M[:, f % (2 if st is early else 1), :, :].rearrange("p t n -> p (t n)")
            return m.rearrange("p (s t n) -> p s t n", s=2, t=NT)

        TG = B * N // 512
        X3 = ADJ[:, 0:4 * B * N].bitcast(F32).rearrange("p (t f) -> p t f", f=F)
        GT = early.vf[:, 0:B * N]
        qrow = early.M[0:3, :, :, :].rearrange("p g t n -> p (g t n)").bitcast(BF16)
        qparts = late.Dn[0:B * NT, 3 * P:5 * P].bitcast(BF16).rearrange("p (q n) -> p q n", q=4)
        qrest = late.Dn[0:B * NT, 5 * P:6 * P]
        tcol = late.Dn[:, 6 * P:6 * P + 3]
        qT = late.Dn[0:B * NT, 0:P]
        K2n = late.Dn[:, 2 * P:2 * P + F]
        ring4 = [early.mps[:, 0, :], early.mps[:, 1, :], late.mps[:, 0, :], late.mps[:, 1, :]]

        USE = {0: dict(T=0, proj=2, rows=10, mean=14), 1: dict(T=15, proj=19, rows=23, mean=25),
               2: dict(T=0, proj=2, rows=5, mean=7), 3: dict(T=8, proj=10, rows=13),
               4: dict(T=15, proj=17, stats=19, q=20, G=21)}
        TILES = {0: 1, 1: 2, 2: 3, 3: 3}
        NTR = {0: 2, 1: 4, 2: 2, 3: 2, 4: 2}
        SLOT = {0: 0, 1: 24, 2: 0, 3: 8, 4: 16}
        LNI = {0: 0, 2: 0, 3: 1, 4: 2}
        NTH = {0: 0, 1: 1, 2: 0, 3: 1}
        HEADS = {0: H, 1: 1, 2: 1, 3: 1}
        BC = {0: 0, 1: 8, 2: 0, 3: 1}
        SEL = {0: 0, 1: 8, 2: 0, 3: 2}
        CUT = {0: 0, 1: 2, 2: 0, 3: 2, 4: 4}
        ELU = {0: 0, 1: 2, 2: 0}

        def part_of(layer, k):
            if layer == 4:
                return slice(0, F)
            s, w = (1 - k if layer == 0 else k), (E if layer == 0 else E1)
            return slice(s * w, (s + 1) * w)

        def waits(eng, name):
            def wait(st, g, signal, k):
                eng.wait_ge(st.S[signal], g.value(st.per[signal], k))

            def alone():
                eng.sem_inc(passed[name], 1)
            return wait, alone

        def run(eng, steps_of):
            def go(steps, base):
                for name, off, *a in steps:
                    if name in steps_of:
                        steps_of[name](base.next(off), *a)

            go(order("C"), Graph(0, -2))
            go(order("AC"), Graph(0, -1))
            with eng.Fori(0, TURNS) as pair:
                if "turn" in steps_of:
                    steps_of["turn"](pair)
                for n in range(2):
                    go(order("LAC"), Graph(pair, n))
            if "turn" in steps_of:
                steps_of["turn"](TURNS)
            go(order("LA"), Graph(0, B - 2))
            go(order("L"), Graph(0, B - 1))

        block = ctx.enter_context(nc.Block())

        @block.sync
        def _(sp):
            wait, alone = waits(sp, "sp")

            def col(v):
                return v.rearrange("(c o) -> c o", o=1)

            def row(v, n):
                return v.rearrange("(o n) -> o n", o=1).to_broadcast([P, n])

            eFb, eHin = early.Fb, early.Hin
            loads = [
                (WX0[:, 0:HD].rearrange("f (h d) -> f h d", h=H), W1.rearrange("h f d -> f h d")),
                (eFb[:, 0, 0:2 * HD], a1.rearrange("(o h) d -> o (h d)", o=1).to_broadcast([P, 2 * HD])),
                (WX1[:, :, 0:F], W2.rearrange("(k p) c -> p k c", p=P)),
                (eFb[:, 1, 0:2 * F], row(a2, 2 * F)),
                (WX2[:, 0:F], gW),
                (eFb[:, 1, 2 * F:4 * F], ga.rearrange("n o -> o n").to_broadcast([P, 2 * F])),
                (eHin[:, 0, :], lW),
                (eFb[:, 0, 2 * HD:2 * HD + 2 * F], row(la, 2 * F)),
                (K1s[:, :], K1), (K2s[:, :], K2), (b1b[:, :], row(b1, F)),
                (cols[:, 0:1], col(gam1)), (cols[:, 1:2], col(bet1)), (cols[:, 2:3], col(b2)),
                (cols[:, 3:4], col(gam2)), (cols[:, 4:5], col(bet2)),
            ]
            assert len(loads) == LOADS
            adj_rows = adj.rearrange("b n m -> (b n) m")
            x_rows = x.rearrange("b n f -> (b n) f")

            def adjacency(g, t):
                if g.off or not isinstance(g.pair, int) or t >= 2:
                    wait(prep, g, "adj_conv", t - 1)
                    alone()
                sp.dma_start(adj_in[:, t % 2, :], adj_rows[bass.ds(g.value(N, t * P), P), :])\
                    .then_inc(adj_land[t % 2], 16)

            def load_x(g):
                sp.dma_start(xres[:, g.par, :, :], x_rows[bass.ds(g.value(N, 0), N), :]
                             .rearrange("(t p) f -> p t f", p=P)).then_inc(x_land[g.par], 16)

            adjacency(Graph(0, 0), 0)
            adjacency(Graph(0, 0), 1)
            for dst, src in loads:
                sp.dma_start(dst, src).then_inc(w_land, 16)
            load_x(Graph(0, 0))
            for t in range(2, NT):
                adjacency(Graph(0, 0), t)
            load_x(Graph(0, 1))
            for t in range(NT):
                adjacency(Graph(0, 1), t)

            def store(g, front):
                if front:
                    for t in range(NT):
                        adjacency(g.next(2), t)
                wait(late, g, "x3_ready", 1)
                alone()
                sp.dma_start(x3_dram[bass.ds(g.value(N, 0), N), :].rearrange("(t p) f -> p t f", p=P),
                             xres[:, g.par, :, :]).then_inc(x3_store, 16)
                if front:
                    sp.wait_ge(x3_store, g.value(16, 16))
                    alone()
                    wait(late, g, "h_ready", 6)
                    alone()
                    load_x(g.next(2))
                wait(late, g, "gen_free", LATE["gen_free"])
                alone()
                sp.dma_start(gt_dram[:, bass.ds(g.value(N, 0), N)], GTs).then_inc(gt_store, 16)

            with sp.Fori(0, TURNS) as pair:
                for n in range(2):
                    store(Graph(pair, n), True)
            store(Graph(0, B - 2), False)
            store(Graph(0, B - 1), False)
            sp.wait_ge(x3_store, 16 * B)
            sp.wait_ge(gt_store, 16 * B)
            sp.wait_ge(t_chain, 1)
            for g in range(TG):
                sp.dma_start(GT[:, g * 512:(g + 1) * 512], gt_dram[:, g * 512:(g + 1) * 512]).then_inc(t_gt[g // 4], 16)
                if g == 3:
                    sp.wait_ge(t_qp, 1)
                    for q in range(3):
                        sp.dma_start(qrow[q:q + 1, :].rearrange("o (k n) -> o k n", n=P), qparts[:, q, :])\
                            .then_inc(t_q, 16)
            sp.dma_start(X3, x3_dram.rearrange("(t p) f -> p t f", p=P)).then_inc(t_x3, 16)
            o_rows = out.rearrange("b n f -> (b n) f").rearrange("(g t p) f -> g p t f", p=P, t=4)
            for g in range(TG):
                sp.wait_ge(t_out, g + 1)
                sp.dma_start(o_rows[g], X3[:, 4 * g:4 * g + 4, :]).then_inc(t_store, 16)
            sp.wait_ge(t_store, 16 * TG)

        @block.gpsimd
        def _(pool):
            wait, alone = waits(pool, "pool")
            nc.gpsimd.memset(ident[:, :], 0.0).then_inc(w_pool, 1)
            nc.gpsimd.memset(ones[:, :], 1.0).then_inc(w_pool, 1)
            nc.gpsimd.memset(mhalf[:, :], -0.5).then_inc(w_pool, 1)
            pool.wait_ge(w_pool, 3)
            nc.gpsimd.affine_select(out=ident[:, :], in_=ident[:, :], compare_op=ALU.not_equal, fill=1.0,
                                    base=0, pattern=[[-1, P]], channel_multiplier=1).then_inc(w_pool, 1)
            pool.wait_ge(w_pool, 4)

            def ln(g, layer, f):
                if f == 0:
                    return
                st = of(layer)
                wait(st, g, "ln_var", LNI[layer] + 1)
                nc.gpsimd.tensor_tensor(st.rstd[:, :], st.ve[:, :], mhalf[:, :], ALU.pow).then_inc(st.S["rstd"], 1)
                wait(st, g, "rstd", LNI[layer] + 1)

            def lin(g, layer, k=0):
                st = of(layer)
                if layer == 0:
                    wait(st, g, "h_ready", 2)
                    nc.gpsimd.tensor_tensor(xres[:, g.par, :, :], xres[:, g.par, :, :], st.Hin, ALU.add)\
                        .then_inc(st.S["res_h"], 1)
                    wait(st, g, "res_h", 1)

            def broadcast(g, layer, h):
                st = of(layer)
                wait(st, g, "gen_free", USE[layer]["rows"] + 2 * (h // 4) + 2)
                if layer == 0 and h >= 2:
                    wait(st, g, "mplus", h - 1)
                alone()
                q = 32 * (h % 4)
                nc.gpsimd.partition_broadcast(st.Fb[:, h % 2, :], st.rows[q:q + 1, h // 4, :])\
                    .then_inc(st.S["bcast"], 1)
                wait(st, g, "bcast", BC[layer] + h + 1)

            def rng(g, layer):
                st, n = of(layer), 2 * HEADS[layer]
                wait(st, g, "f2_range", NTH[layer] + 1)
                alone()
                nc.gpsimd.partition_all_reduce(st.f2g[:, 0:n], st.f2r[:, 0:n], P, RMAX).then_inc(st.S["f2_gmax"], 1)
                wait(st, g, "f2_gmax", NTH[layer] + 1)
                broadcast(g, layer, 0)

            def sel(g, layer, h):
                if layer == 0 and h + 1 < H:
                    broadcast(g, layer, h + 1)

            def a8(g, t):
                if g.off >= 2 and t == 0:
                    wait(late, g.next(-2), "slot_full", LATE["slot_full"])
                wait(prep, g, "adj_conv", t + 1)
                alone()
                nc.gpsimd.tensor_copy(A8[:, g.par, t, :], A16[:, t, :], saturate=False).then_inc(prep.S["a8_done"], 1)
                wait(prep, g, "a8_done", t + 1)

            run(pool, dict(ln=ln, lin=lin, rng=rng, sel=sel, a8=a8))
            for k in range(2):
                pool.wait_ge(t_var, k + 1)
                nc.gpsimd.tensor_tensor(sc[:, 2 + 8 * k:3 + 8 * k], sc[:, 1 + 8 * k:2 + 8 * k], mhalf[:, 0:1],
                                        ALU.pow).then_inc(t_rstd, 1)

        @block.scalar
        def _(act):
            wait, alone = waits(act, "act")

            def drain(g, layer, kind, k, dst, width, accum=None):
                st = of(layer)
                use = USE[layer][kind] + k
                wait(st, g, "gen_full", use + 1)
                src = st.gen[0:dst.shape[0], use % st.banks, 0:width]
                if len(dst.shape) == 3:
                    src = src.rearrange("p (t c) -> p t c", c=dst.shape[2])
                if accum is None:
                    nc.scalar.activation(dst, src, ACT.Copy).then_inc(st.S["gen_free"], 1)
                else:
                    nc.scalar.activation(dst, src, ACT.Copy, accum_out=accum).then_inc(st.S["gen_free"], 1)

            def conv(g, t):
                if t == 0 and g.off >= 1:
                    before = g.next(-1)
                    wait(prep, before, "at_full", NT)
                    wait(prep, before, "a8_done", NT)
                    wait(prep, before, "deg_ready", 1)
                act.wait_ge(adj_land[t % 2], g.value(16 * HT, 16 * (t // 2 + 1)))
                nc.scalar.activation(A16[:, t, :], adj_in[:, t % 2, :], ACT.Copy,
                                     accum_out=deg[:, t:t + 1]).then_inc(prep.S["adj_conv"], 1)

            def tr(g, u):
                wait(prep, g, "at_full", u + 1)
                if u == 0 and g.off >= 1:
                    wait(prep, g.next(-1), "deg_ready", 1)
                alone()
                nc.scalar.activation(AT[:, g.par, u, :], tps[:, :], ACT.Copy,
                                     accum_out=cnt[:, u:u + 1], saturate=False).then_inc(prep.S["at_ready"], 1)

            def lin(g, layer, k=0):
                st = of(layer)
                if layer == 1:
                    wait(early, g, "bcast", 8)
                    for f in range(2):
                        drain(g, 1, "T", 2 * k + f, xcT[:, k, f * HALF:(f + 1) * HALF], HALF,
                              st.csum[:, 2 * k + f:2 * k + f + 1])
                    return
                wait(st, g, "nmr", LNI[layer] + 1)
                for t in range(NT):
                    last = nc.scalar.activation(st.Hin[:, t, :], xres[:, g.par, t, :], ACT.Relu,
                                                bias=st.nmr[:, t:t + 1], scale=st.rstd[:, t:t + 1])
                    if t % HT == HT - 1:
                        last.then_inc(st.S["h_ready"], 1)
                for f in range(2):
                    drain(g, layer, "T", f, st.hT[:, f * HALF:(f + 1) * HALF], HALF, st.csum[:, f:f + 1])

            def proj(g, layer):
                st = of(layer)
                Hv, width, n = (Hn0, C0, 1) if layer == 0 else (st.Hn1, C1, TILES[layer])
                for k, t in enumerate(range(0, NT, n)):
                    m = min(n, NT - t)
                    drain(g, layer, "proj", k, Hv[:, t:t + m, :], m * width)

            def rows(g, layer):
                st = of(layer)
                for r in range(2 if layer == 0 else 1):
                    for f in range(2):
                        drain(g, layer, "rows", 2 * r + f,
                              st.rows[0:(P if layer == 0 else 1), r, f * HALF:(f + 1) * HALF], HALF)

            def mean(g, layer):
                w = HD if layer == 0 else F
                drain(g, layer, "mean", 0, of(layer).meanb[:, 0:w], w)

            def rng(g, layer):
                st, n = of(layer), NT * HEADS[layer]
                wait(st, g, "args", NTH[layer] + 1)
                nc.scalar.activation(st.fac[:, :, 0:n], st.args[:, :, 0:n], ACT.Exp).then_inc(st.S["exps"], 1)

            def cut1(g, layer, k):
                st, c = of(layer), part_of(layer, k)
                Vt, Ft = parts_of(layer)
                if layer == 4 and k == 0:
                    wait(late, g, "gen_free", USE[4]["proj"] + 2)
                else:
                    wait(st, g, "v_full", min(CUT[layer] + k + 1, st.per["v_full"]))
                nc.scalar.activation(Vt[:, :, 0, c], Ft[:, :, c], ACT.Copy).then_inc(st.S["v_hi"], 1)

            def cut2(g, layer, k):
                st, c = of(layer), part_of(layer, k)
                Vt, Ft = parts_of(layer)
                wait(st, g, "v_rest", CUT[layer] + k + 1)
                nc.scalar.activation(Vt[:, :, 1, c], Ft[:, :, c], ACT.Copy).then_inc(st.S["v_mid"], 1)

            def sel(g, layer, h):
                st = of(layer)
                if layer == 0:
                    wait(st, g, "bcast", h + 1)
                    if h >= 2:
                        wait(st, g, "slot_full", NT + 2 * (h - 1))
                    alone()
                    for t in range(DVE_CMP, NT):
                        k = t * H + h
                        last = nc.scalar.activation(st.M[:, h % 2, t, :].bitcast(U8), st.Fb[:, h % 2, :], ACT.Relu,
                                                    bias=st.bigf2[:, k:k + 1], scale=STEP_GAIN)
                else:
                    wait(st, g, "bcast", BC[layer] + 1)
                    if h and st is late:
                        wait(st, g, "slot_full", SLOT[layer] + HT)
                    alone()
                    for t in range(DVE_CMP, NT):
                        last = nc.scalar.activation(halves(st, h)[:, 0, t, :].bitcast(U8),
                                                    st.Fb[:, 0, h * HALF:(h + 1) * HALF], ACT.Relu,
                                                    bias=st.bigf2[:, t:t + 1], scale=STEP_GAIN)
                last.then_inc(st.S["act_cmp"], 1)

            def mask(g, i):
                wait(early, g, "slot_full", i + 1)
                if i == 0:
                    wait(early, g, "res_h", 1)
                nc.scalar.activation(D0[:, i, :, :].rearrange("p h c -> p (h c)"), early.mps[:, i % 2, 0:H * E],
                                     ACT.Copy).then_inc(early.S["act_slot"], 1)

            def head(g, h, f):
                k = NT + 2 * h + f
                wait(early, g, "slot_full", k + 1)
                nc.scalar.activation(Vf0[:, HT * f:HT * (f + 1), h, :],
                                     early.mps[:, k % 2, 0:HT * 2 * E].rearrange("p (t c) -> p t c", t=HT),
                                     ACT.Copy).then_inc(early.S["act_slot"], 1)

            def slot(g, layer, i):
                st, k = of(layer), SLOT[layer] + i
                wait(st, g, "slot_full", k + 1)
                nc.scalar.activation(st.Vf1[:, i, :], st.mps[:, k % 2, 0:2 * E1], ACT.Copy)\
                    .then_inc(st.S["act_slot"], 1)

            def elu(g, layer, k=0):
                st = of(layer)
                wait(st, g, "mneg", ELU[layer] + k + 1)
                src = ex0[:, :, k, :] if layer == 0 else st.ex1[:, HT * k:HT * (k + 1), :]
                nc.scalar.activation(src, src, ACT.Exp).then_inc(st.S["eexp"], 1)

            def comb3(g, k):
                elu(g, 0, k)

            def post3(g, layer, f):
                if layer < 3:
                    elu(g, layer, f)

            def gproj(g):
                for f in range(2):
                    drain(g, 4, "proj", f, late.Vf[:, f * HALF:(f + 1) * HALF], HALF)

            def gagg(g, i):
                k = SLOT[4] + i
                wait(late, g, "slot_full", k + 1)
                nc.scalar.activation(region[:, i, :], late.mps[:, k % 2, 0:F], ACT.Copy,
                                     scale=rc[:, g.par, i:i + 1]).then_inc(late.S["act_slot"], 1)

            def gstat(g):
                drain(g, 4, "stats", 0, bn_g[:, :], 2)

            def gq(g):
                drain(g, 4, "q", 0, q3[:, :, :].rearrange("p t q -> p (t q)"), NT * 3)

            def gout(g):
                for f in range(2):
                    drain(g, 4, "G", f, GTs[:, f * HALF:(f + 1) * HALF], HALF)

            act.wait_ge(w_pe, 1)
            nc.scalar.activation(WX3[:, 0:F], early.gen[:, 0, 0:F], ACT.Copy).then_inc(w_act, 1)
            run(act, dict(conv=conv, tr=tr, lin=lin, proj=proj, rows=rows, mean=mean, gq=gq, rng=rng, cut1=cut1, cut2=cut2, sel=sel, mask=mask,
                          head=head, slot=slot, comb3=comb3, post3=post3, gproj=gproj, gagg=gagg, gstat=gstat, gout=gout))
            act.wait_ge(t_peq, 1)
            nc.scalar.activation(qT, late.gen[0:B * NT, 0, 0:P], ACT.Copy).then_inc(t_qT, 1)
            act.wait_ge(t_petk, 1)
            nc.scalar.activation(tK2[:, :], early.gen[0:3, 0, 0:F], ACT.Copy).then_inc(t_tK2, 1)
            for g in range(TG):
                act.wait_ge(t_full, g + 1)
                nc.scalar.activation(GT[:, g * 512:(g + 1) * 512], ring4[g % 4], ACT.Identity,
                                     bias=cols[:, 2:3]).then_inc(t_kept, 1)
            act.wait_ge(t_scale, 2)
            for g in range(TG):
                nc.scalar.activation(GT[:, g * 512:(g + 1) * 512], GT[:, g * 512:(g + 1) * 512], ACT.Identity,
                                     bias=sc[:, 12:13], scale=sc[:, 11:12]).then_inc(t_norm, 1)

        @block.vector
        def _(dve):
            wait, alone = waits(dve, "dve")
            dve.wait_ge(w_land, 16 * LOADS)
            dve.wait_ge(w_pool, 4)
            done = [0]

            def setup(ins):
                done[0] += 1
                ins.then_inc(w_dve, 1)
                dve.wait_ge(w_dve, done[0])

            setup(nc.vector.tensor_copy(identb[:, :], ident[:, :]))
            setup(nc.vector.memset(WR0[:, :, :], 0.0))
            setup(nc.vector.memset(bnacc[:, :], 0.0))
            prod = late.Dn[:, 0:HD].rearrange("p (h d) -> p h d", h=H)
            a1b = early.Fb[:, 0, 0:2 * HD].rearrange("p (h s d) -> p h s d", h=H, s=2)
            for s in range(2):
                setup(nc.vector.tensor_tensor(prod, WX0[:, 0:HD].rearrange("f (h d) -> f h d", h=H),
                                              a1b[:, :, s, :], ALU.mult))
                setup(nc.vector.tensor_reduce(WX0[:, HD + s * H:HD + (s + 1) * H], prod, AX_X, ALU.add))
            for g in range(2):
                setup(nc.vector.tensor_copy(WR0[:, g, :].rearrange("p (q c) -> p q c", q=4)[:, :, 0],
                                            WX0[:, HD + 4 * g:HD + 4 * g + 4]))
            dve.wait_ge(w_act, 1)
            for W, avec in ((WX1[:, 0, :], early.Fb[:, 1, 0:2 * F]), (WX1[:, 1, :], early.Fb[:, 1, 0:2 * F]),
                            (WX2[:, :], early.Fb[:, 1, 2 * F:4 * F]),
                            (WX3[:, :], early.Fb[:, 0, 2 * HD:2 * HD + 2 * F])):
                for s in range(2):
                    setup(nc.vector.tensor_tensor(late.Dn[:, 0:F], W[:, 0:F], avec[:, s * F:(s + 1) * F], ALU.mult))
                    setup(nc.vector.tensor_reduce(W[:, F + s:F + s + 1], late.Dn[:, 0:F], AX_X, ALU.add))

            turn_at, steps = [None], [0]

            def turn(pair):
                assert steps[0] == (CHAIN_FIRST if turn_at[0] is None else CHAIN_TURN), steps[0]
                turn_at[0], steps[0] = pair, 0

            def go(ins):
                steps[0] += 1
                ins.then_inc(dve_chain, 1)

            def sync():
                if turn_at[0] is None:
                    dve.wait_ge(dve_chain, steps[0])
                else:
                    dve.wait_ge(dve_chain, turn_at[0] * CHAIN_TURN + (CHAIN_FIRST + steps[0]))

            def link(ins):
                go(ins)
                sync()

            def signal(st, name):
                dve.sem_inc(st.S[name], 1)

            def degrees(g):
                e, r, r3 = emp[:, g.par, :], rc[:, g.par, :], rc3[:, g.par, :, :]
                wait(prep, g, "at_ready", NT)
                if g.off >= 2:
                    wait(late, g.next(-2), "gen_free", LATE["gen_free"])
                link(nc.vector.tensor_scalar(e, deg[:, :], 0.0, None, ALU.is_equal))
                link(nc.vector.tensor_scalar(rcr[:, :], cnt[:, :], 1.0, None, ALU.max))
                link(nc.vector.reciprocal(r, rcr[:, :]))
                link(nc.vector.tensor_copy(r3[:, :, 0], r))
                link(nc.vector.tensor_tensor(rcr[:, :], r, r3[:, :, 0], ALU.subtract))
                link(nc.vector.tensor_copy(r3[:, :, 1], rcr[:, :]))
                link(nc.vector.tensor_tensor(r3[:, :, 2], rcr[:, :], r3[:, :, 1], ALU.subtract))
                signal(prep, "deg_ready")

            def ln(g, layer, f):
                st = of(layer)
                if layer == 0 and f == 0:
                    dve.wait_ge(x_land[g.par], g.pair * 16 + (16 * (g.off // 2) + 16))
                for t in range(HT * f, HT * (f + 1)):
                    go(nc.vector.bn_stats(st.st6[:, t, :], xres[:, g.par, t, :]))
                sync()
                alone()
                for t in range(HT * f, HT * (f + 1)):
                    go(nc.vector.bn_aggr(st.mv[:, t, :], st.st6[:, t, :]))
                if f:
                    sync()
                    link(nc.vector.tensor_scalar(st.ve[:, :], st.mv[:, :, 1], LN_EPS, None, ALU.add))
                    signal(st, "ln_var")

            def lin(g, layer, k=0):
                if layer == 1:
                    return
                st = of(layer)
                wait(st, g, "rstd", LNI[layer] + 1)
                link(nc.vector.scalar_tensor_tensor(st.nmr[:, :], st.mv[:, :, 0], -1.0, st.rstd[:, :],
                                                    ALU.mult, ALU.mult))
                signal(st, "nmr")

            def rows(g, layer):
                if layer == 3:
                    return
                st = of(layer)
                wait(st, g, "gen_free", USE[layer]["T"] + NTR[layer])
                for k in range(NTR[layer] // 2):
                    link(nc.vector.tensor_tensor(st.csum[:, 2 * k:2 * k + 1], st.csum[:, 2 * k:2 * k + 1],
                                                 st.csum[:, 2 * k + 1:2 * k + 2], ALU.add))
                    link(nc.vector.tensor_scalar(st.mean_lhs[:, k, :], ones[:, :], st.csum[:, 2 * k:2 * k + 1],
                                                 1.0 / N, ALU.mult, ALU.mult))
                signal(st, "mean_lhs")

            def rng(g, layer):
                st, heads = of(layer), HEADS[layer]
                n = NT * heads
                Hv, c = (Hn0, HD) if layer == 0 else (st.Hn1, F)
                f1, f2 = Hv[:, :, c:c + heads], Hv[:, :, c + heads:c + 2 * heads]

                def v3(ap):
                    return ap.rearrange("p (t h) -> p t h", h=heads)

                wait(st, g, "gen_free", USE[layer]["rows"])
                f2_ht = f2.rearrange("p t h -> p h t")
                lo = st.f2r[:, heads:2 * heads]
                go(nc.vector.tensor_reduce(st.f2r[:, 0:heads], f2_ht, AX_X, ALU.max))
                link(nc.vector.tensor_reduce(lo, f2_ht, AX_X, ALU.min))
                link(nc.vector.tensor_scalar(lo, lo, -1.0, None, ALU.mult))
                signal(st, "f2_range")
                go(nc.vector.tensor_scalar(v3(st.nf2[:, 0:n]), f2, -1.0, None, ALU.mult))
                go(nc.vector.tensor_scalar(v3(st.bigf2[:, 0:n]), f2, STEP_GAIN, None, ALU.mult))
                wait(st, g, "f2_gmax", NTH[layer] + 1)
                link(nc.vector.tensor_tensor(st.Cb[:, 0:heads], st.f2g[:, 0:heads], st.f2g[:, heads:2 * heads],
                                             ALU.subtract))
                link(nc.vector.tensor_scalar(st.Cb[:, 0:heads], st.Cb[:, 0:heads], 0.5, None, ALU.mult))
                Cv = st.Cb[:, 0:heads].rearrange("p (o h) -> p o h", o=1).to_broadcast([P, NT, heads])
                go(nc.vector.tensor_tensor(v3(st.sarg[:, 0:n]), f1, Cv, ALU.add))
                link(nc.vector.tensor_tensor(v3(st.args[:, 2, 0:n]), f2, Cv, ALU.subtract))
                go(nc.vector.tensor_scalar(st.args[:, 0, 0:n], st.sarg[:, 0:n], 1.0 - SLOPE, 0.0, ALU.mult, ALU.min))
                go(nc.vector.tensor_scalar(st.args[:, 1, 0:n], st.sarg[:, 0:n], SLOPE - 1.0, 0.0, ALU.mult, ALU.min))
                link(nc.vector.tensor_scalar(st.args[:, 3, 0:n], st.args[:, 2, 0:n], SLOPE, None, ALU.mult))
                signal(st, "args")

            def val(g, layer, k):
                st, heads = of(layer), HEADS[layer]
                n = NT * heads
                wait(st, g, "exps", NTH[layer] + 1)
                wait(st, g, "bcast", BC[layer] + 1)
                w = D if layer == 0 else F
                s = 1 - k if layer == 0 else k
                o = s * (w + 1)
                if layer == 0:
                    dst = Vf0[:, :, :, o:o + w]
                    values = Hn0[:, :, 0:HD].rearrange("p t (h d) -> p t h d", h=H)
                    cf = st.fac[:, 2 + s, 0:n].rearrange("p (t h o) -> p t h o", h=H, o=1)\
                        .to_broadcast([P, NT, H, D])
                    one = Vf0[:, :, :, o + w]
                    cv = st.fac[:, 2 + s, 0:n].rearrange("p (t h) -> p t h", h=H)
                else:
                    dst = st.Vf1[:, :, o:o + w]
                    values = st.Hn1[:, :, 0:F]
                    cf = st.fac[:, 2 + s, 0:n].rearrange("p (t o) -> p t o", o=1).to_broadcast([P, NT, F])
                    one = st.Vf1[:, :, o + w]
                    cv = st.fac[:, 2 + s, 0:n]
                go(nc.vector.tensor_tensor(dst, values, cf, ALU.mult))
                go(nc.vector.tensor_copy(one, cv))
                sync()
                signal(st, "v_full")

            def cut1(g, layer, k):
                st, c = of(layer), part_of(layer, k)
                Vt, Ft = parts_of(layer)
                wait(st, g, "v_hi", CUT[layer] + k + 1)
                link(nc.vector.tensor_tensor(Ft[:, :, c], Ft[:, :, c], Vt[:, :, 0, c], ALU.subtract))
                signal(st, "v_rest")

            def cut2(g, layer, k):
                st, c = of(layer), part_of(layer, k)
                Vt, Ft = parts_of(layer)
                wait(st, g, "v_mid", CUT[layer] + k + 1)
                link(nc.vector.tensor_tensor(Vt[:, :, 2, c], Ft[:, :, c], Vt[:, :, 1, c], ALU.subtract))
                signal(st, "v_ready")

            def sel(g, layer, h):
                st = of(layer)
                if layer == 0:
                    wait(st, g, "bcast", h + 1)
                    if h >= 2:
                        wait(st, g, "slot_full", NT + 2 * (h - 1))
                    alone()
                    for t in range(DVE_CMP):
                        k = t * H + h
                        go(nc.vector.tensor_scalar(st.M[:, h % 2, t, :], st.Fb[:, h % 2, :], st.nf2[:, k:k + 1],
                                                   None, ALU.is_ge, saturate=False))
                    sync()
                    wait(st, g, "act_cmp", h + 1)
                    for f in range(2):
                        m = st.M[:, h % 2, HT * f:HT * (f + 1), :].bitcast(U32)
                        a = AT[:, g.par, HT * f:HT * (f + 1), :].bitcast(U32)
                        go(nc.vector.tensor_tensor(m, m, a, ALU.bitwise_and))
                    sync()
                    signal(st, "mplus")
                else:
                    wait(st, g, "bcast", BC[layer] + 1)
                    if h and st is late:
                        wait(st, g, "slot_full", SLOT[layer] + HT)
                    alone()
                    mh = halves(st, h)
                    for t in range(DVE_CMP):
                        go(nc.vector.tensor_scalar(mh[:, 0, t, :], st.Fb[:, 0, h * HALF:(h + 1) * HALF],
                                                   st.nf2[:, t:t + 1], None, ALU.is_ge, saturate=False))
                    sync()
                    wait(st, g, "act_cmp", SEL[layer] + h + 1)
                    a = AT[:, g.par, :, h * HALF:(h + 1) * HALF].bitcast(U32)
                    plus, minus = mh[:, 0, :, :].bitcast(U32), mh[:, 1, :, :].bitcast(U32)
                    link(nc.vector.tensor_tensor(plus, plus, a, ALU.bitwise_and))
                    signal(st, "mplus")
                    link(nc.vector.tensor_tensor(minus, plus, a, ALU.bitwise_xor))
                    signal(st, "mminus")

            def means(g, layer, o_all, mean, ts=slice(0, NT)):
                st = of(layer)
                wait(st, g, "gen_free", USE[layer]["mean"] + 1)
                for t in range(ts.start, ts.stop):
                    go(nc.vector.scalar_tensor_tensor(o_all[:, t, :], mean, emp[:, g.par, t:t + 1],
                                                      o_all[:, t, :], ALU.mult, ALU.add))
                sync()

            def comb1(g, k):
                wait(early, g, "act_slot", 2 * NT + NT * k)
                hs = slice(HT * k, HT * (k + 1))
                num, Ub, Ud = D0[:, :, hs, :], Vf0[:, :, hs, 0:E], Vf0[:, :, hs, E:2 * E]

                def rows_factor(s):
                    f = early.fac[:, s, 0:NT * H].rearrange("p (t h o) -> p t h o", h=H, o=1)
                    return f[:, :, hs, :].to_broadcast([P, NT, HT, E])

                link(nc.vector.tensor_tensor(num, num, Ud, ALU.subtract))
                go(nc.vector.tensor_tensor(Ub, Ub, rows_factor(0), ALU.mult))
                link(nc.vector.tensor_tensor(num, num, rows_factor(1), ALU.mult))
                link(nc.vector.tensor_tensor(num, num, Ub, ALU.add))

            def comb2(g, k):
                hs, c = slice(HT * k, HT * (k + 1)), slice(P * k, P * (k + 1))
                ev = emp[:, g.par, :].rearrange("p (t o) -> p t o", o=1).to_broadcast([P, NT, HT])
                rden = early.rden[:, 0:NT * HT]
                link(nc.vector.tensor_tensor(rden.rearrange("p (t h) -> p t h", h=HT), D0[:, :, hs, D], ev, ALU.add))
                link(nc.vector.reciprocal(rden, rden))
                rv = rden.rearrange("p (t h o) -> p t h o", h=HT, o=1).to_broadcast([P, NT, HT, D])
                xh = xc[:, :, c].rearrange("p t (h d) -> p t h d", h=HT)
                link(nc.vector.tensor_tensor(xh, D0[:, :, hs, 0:D], rv, ALU.mult))
                means(g, 0, xc[:, :, c], early.meanb[:, c])
                link(nc.vector.tensor_scalar(ex0[:, :, k, :], xc[:, :, c], 0.0, None, ALU.min))
                signal(early, "mneg")

            def comb3(g, k):
                xk = xc[:, :, P * k:P * (k + 1)]
                wait(early, g, "eexp", k + 1)
                link(nc.vector.scalar_tensor_tensor(xk, ex0[:, :, k, :], -1.0, xk, ALU.add, ALU.max))
                signal(early, "xc_ready")

            def post1(g, layer, f):
                st, ts = of(layer), slice(HT * f, HT * (f + 1))
                wait(st, g, "act_slot", SLOT[layer] + HT * (f + 1))
                Ub, Ud = st.Vf1[:, ts, 0:E1], st.Vf1[:, ts, E1:2 * E1]
                ca = st.fac[:, 0, ts].rearrange("p (n o) -> p n o", o=1).to_broadcast([P, HT, E1])
                cc = st.fac[:, 1, ts].rearrange("p (n o) -> p n o", o=1).to_broadcast([P, HT, E1])
                go(nc.vector.tensor_tensor(Ub, Ub, ca, ALU.mult))
                link(nc.vector.tensor_tensor(Ud, Ud, cc, ALU.mult))
                link(nc.vector.tensor_tensor(Ub, Ub, Ud, ALU.add))

            def post2(g, layer, f):
                st, ts = of(layer), slice(HT * f, HT * (f + 1))
                rden = st.rden[:, ts]
                link(nc.vector.tensor_tensor(rden, st.Vf1[:, ts, F], emp[:, g.par, ts], ALU.add))
                link(nc.vector.reciprocal(rden, rden))
                rv = rden.rearrange("p (t o) -> p t o", o=1).to_broadcast([P, HT, F])
                link(nc.vector.tensor_tensor(st.O1[:, ts, :], st.Vf1[:, ts, 0:F], rv, ALU.mult))
                if layer < 3:
                    means(g, layer, st.O1, st.meanb[:, 0:F], ts)
                    link(nc.vector.tensor_scalar(st.ex1[:, ts, :], st.O1[:, ts, :], 0.0, None, ALU.min))
                    signal(st, "mneg")

            def post3(g, layer, f):
                st, ts = of(layer), slice(HT * f, HT * (f + 1))
                xr, o1 = xres[:, g.par, ts, :], st.O1[:, ts, :]
                if layer < 3:
                    wait(st, g, "eexp", ELU[layer] + f + 1)
                    link(nc.vector.scalar_tensor_tensor(o1, st.ex1[:, ts, :], -1.0, o1, ALU.add, ALU.max))
                link(nc.vector.tensor_tensor(xr, xr, o1, ALU.add))
                if layer == 3 and f:
                    signal(late, "x3_ready")

            def greg(g):
                wait(late, g, "act_slot", LATE["act_slot"])
                bb = b1b[:, :].rearrange("p (o c) -> p o c", o=1).to_broadcast([P, NT, F])
                link(nc.vector.tensor_tensor(region, region, bb, ALU.add))
                rv = rc[:, g.par, :].rearrange("p (t o) -> p t o", o=1).to_broadcast([P, NT, F])
                go(nc.vector.tensor_tensor(Vf3, region, rv, ALU.mult))
                go(nc.vector.tensor_tensor(square, region, region, ALU.mult))
                sync()
                signal(late, "v_full")
                signal(late, "region")

            def gend(g):
                wait(late, g, "gen_free", USE[4]["q"] + 1)
                go(nc.vector.tensor_tensor(bnacc[:, :], bnacc[:, :], bn_g[:, :], ALU.add))
                link(nc.vector.tensor_reduce(Qall[:, bass.ds(g.value(NT, 0), NT)], q3[:, :, :], AX_X, ALU.add))
                wait(late, g, "gen_free", LATE["gen_free"])
                dve.wait_ge(gt_store, g.value(16, 16))

            run(dve, dict(turn=turn, degrees=degrees, ln=ln, lin=lin, rows=rows, rng=rng, val=val, cut1=cut1, cut2=cut2, sel=sel,
                          comb1=comb1, comb2=comb2, comb3=comb3, post1=post1, post2=post2, post3=post3, greg=greg, gend=gend))

            tick = [0]

            def tgo(ins):
                tick[0] += 1
                ins.then_inc(t_chain, 1)

            def tlink(ins):
                tgo(ins)
                dve.wait_ge(t_chain, tick[0])

            tlink(nc.vector.tensor_scalar(sc[:, 4:6], bnacc[:, :], 1.0 / (B * N), None, ALU.mult))
            tlink(nc.vector.tensor_tensor(sc[:, 6:7], sc[:, 4:5], sc[:, 4:5], ALU.mult))
            tlink(nc.vector.scalar_tensor_tensor(sc[:, 1:2], sc[:, 6:7], -1.0, sc[:, 5:6], ALU.mult, ALU.add))
            tlink(nc.vector.tensor_scalar(sc[:, 1:2], sc[:, 1:2], BN_EPS, None, ALU.add))
            dve.sem_inc(t_var, 1)
            dve.wait_ge(t_rstd, 1)
            tlink(nc.vector.tensor_tensor(sc[:, 7:8], sc[:, 2:3], cols[:, 0:1], ALU.mult))
            tlink(nc.vector.tensor_tensor(sc[:, 6:7], sc[:, 4:5], sc[:, 7:8], ALU.mult))
            tlink(nc.vector.tensor_tensor(sc[:, 8:9], cols[:, 1:2], sc[:, 6:7], ALU.subtract))
            tlink(nc.vector.tensor_scalar(K2n, K2s[:, :], sc[:, 7:8], None, ALU.mult))
            tlink(nc.vector.tensor_scalar(tcol, ones[:, 0:3], sc[:, 8:9], None, ALU.mult))
            dve.sem_inc(t_scale, 1)

            def split(parts, full, rest):
                tlink(nc.vector.tensor_copy(parts[:, 0, :], full))
                tlink(nc.vector.tensor_tensor(rest, full, parts[:, 0, :], ALU.subtract))
                tlink(nc.vector.tensor_copy(parts[:, 1, :], rest))
                tlink(nc.vector.tensor_tensor(parts[:, 2, :], rest, parts[:, 1, :], ALU.subtract))

            dve.wait_ge(t_qT, 1)
            split(qparts, qT, qrest)
            dve.sem_inc(t_qp, 1)
            dve.wait_ge(t_tK2, 1)
            split(tK2p, tK2[:, :], qrest[0:3, :])
            dve.sem_inc(t_tp, 1)
            for g in range(TG):
                dve.wait_ge(t_kept, g + 1)
                tgo(nc.vector.bn_stats(bst[:, g, :], GT[:, g * 512:(g + 1) * 512]))
            dve.wait_ge(t_chain, tick[0])
            tlink(nc.vector.bn_aggr(sc[:, 4:6], bst[:, :, :].rearrange("p g s -> p (g s)")))
            tlink(nc.vector.tensor_scalar(sc[:, 9:10], sc[:, 5:6], BN_EPS, None, ALU.add))
            dve.sem_inc(t_var, 1)
            dve.wait_ge(t_rstd, 2)
            tlink(nc.vector.tensor_tensor(sc[:, 11:12], sc[:, 10:11], cols[:, 3:4], ALU.mult))
            tlink(nc.vector.tensor_tensor(sc[:, 6:7], sc[:, 4:5], sc[:, 11:12], ALU.mult))
            tlink(nc.vector.tensor_tensor(sc[:, 12:13], cols[:, 4:5], sc[:, 6:7], ALU.subtract))
            dve.sem_inc(t_scale, 1)
            dve.wait_ge(t_x3, 16)
            Xg = X3.rearrange("p t f -> p (t f)").rearrange("p (g c) -> p g c", c=512)
            for g in range(TG):
                dve.wait_ge(t_back, g + 1)
                nc.vector.tensor_tensor(Xg[:, g, :], Xg[:, g, :], ring4[g % 4], ALU.add).then_inc(t_out, 1)

        @block.tensor
        def _(pe):
            wait, alone = waits(pe, "pe")
            WX = {0: [WX0[:, :]], 1: [WX1[:, 0, :], WX1[:, 1, :]], 2: [WX2[:, :]], 3: [WX3[:, :]]}
            chunks = {0: [early.hT], 1: [xcT[:, 0, :], xcT[:, 1, :]], 2: [late.hT], 3: [late.hT], 4: [late.hT]}

            def bank(g, layer, kind, k):
                st = of(layer)
                use = USE[layer][kind] + k
                if use >= st.banks:
                    wait(st, g, "gen_free", use - st.banks + 1)
                return st.gen[:, use % st.banks, :]

            def full(last, layer):
                last.then_inc(of(layer).S["gen_full"], 1)

            def tr(g, u):
                wait(prep, g, "adj_conv", NT)
                if u:
                    wait(prep, g, "at_ready", u)
                elif g.off >= 1:
                    wait(prep, g.next(-1), "at_ready", NT)
                for t in range(NT):
                    last = nc.tensor.transpose(tps[:, t * P:(t + 1) * P], A16[:, t, u * P:(u + 1) * P], identb[:, :])
                last.then_inc(prep.S["at_full"], 1)

            def lin(g, layer, k=0):
                if layer == 1:
                    wait(early, g, "xc_ready", k + 1)
                for f in range(2):
                    if layer != 1:
                        wait(of(layer), g, "h_ready", 2 * LNI[layer] + f + 1)
                    o = bank(g, layer, "T", 2 * k + f)
                    for t in range(HT):
                        src = xc[:, HT * f + t, k * P:(k + 1) * P] if layer == 1 else of(layer).Hin[:, HT * f + t, :]
                        last = nc.tensor.transpose(o[:, t * P:(t + 1) * P], src, ident[:, :])
                    full(last, layer)

            def proj(g, layer):
                st, nk, ch = of(layer), len(chunks[layer]), chunks[layer]
                wait(st, g, "gen_free", USE[layer]["T"] + NTR[layer])
                width, n = (C0, 1) if layer == 0 else (C1, TILES[layer])
                for b, t0 in enumerate(range(0, NT, n)):
                    o = bank(g, layer, "proj", b)
                    for t in range(t0, min(NT, t0 + n)):
                        for k in range(nk):
                            last = nc.tensor.matmul(o[:, (t - t0) * width:(t - t0 + 1) * width],
                                                    ch[k][:, t * P:(t + 1) * P], WX[layer][k],
                                                    start=(k == 0), stop=(k == nk - 1))
                    full(last, layer)

            def rows(g, layer):
                nk, ch = len(chunks[layer]), chunks[layer]
                for r in range(2 if layer == 0 else 1):
                    for f in range(2):
                        o = bank(g, layer, "rows", 2 * r + f)
                        for k in range(nk):
                            if layer == 0:
                                last = nc.tensor.matmul(o, WR0[:, r, :], ch[0][:, f * HALF:(f + 1) * HALF],
                                                        start=True, stop=True)
                            else:
                                last = nc.tensor.matmul(o[0:1, :], WX[layer][k][:, F:F + 1],
                                                        ch[k][:, f * HALF:(f + 1) * HALF],
                                                        start=(k == 0), stop=(k == nk - 1))
                        full(last, layer)

            def mean(g, layer):
                st, nk = of(layer), len(chunks[layer])
                wait(st, g, "mean_lhs", NTH[layer] + 1)
                w = HD if layer == 0 else F
                o = bank(g, layer, "mean", 0)
                for k in range(nk):
                    last = nc.tensor.matmul(o[:, 0:w], st.mean_lhs[:, k, :], WX[layer][k][:, 0:w],
                                            start=(k == 0), stop=(k == nk - 1))
                full(last, layer)

            def mask(g, i):
                if i == 0:
                    wait(early, g, "v_ready", 1)
                    wait(prep, g, "at_ready", NT)
                else:
                    wait(early, g, "act_slot", max(i - 1, 1))
                alone()
                for j in range(NT):
                    for q in range(3):
                        last = nc.tensor.matmul(early.mps[:, i % 2, 0:H * E], AT[:, g.par, j, i * P:(i + 1) * P],
                                                V0[:, j, :, q, E:2 * E], start=(j == 0 and q == 0),
                                                stop=(j == NT - 1 and q == 2))
                last.then_inc(early.S["slot_full"], 1)

            def head(g, h, f):
                if f == 0:
                    wait(early, g, "mplus", h + 1)
                if h == 0 and f == 0:
                    wait(early, g, "v_ready", 2)
                k = NT + 2 * h + f
                wait(early, g, "act_slot", k - 1)
                alone()
                for i in range(HT):
                    for j in range(NT):
                        for q in range(3):
                            last = nc.tensor.matmul(
                                early.mps[:, k % 2, i * 2 * E:(i + 1) * 2 * E],
                                early.M[:, h % 2, j, (HT * f + i) * P:(HT * f + i + 1) * P],
                                V0[:, j, h, q, :], start=(j == 0 and q == 0), stop=(j == NT - 1 and q == 2))
                last.then_inc(early.S["slot_full"], 1)

            def slot(g, layer, i):
                st, k, f = of(layer), SLOT[layer] + i, i // HT
                if k >= 2:
                    wait(st, g, "act_slot", k - 1)
                for s, selected in ((0, "mplus"), (1, "mminus")):
                    if i == 0:
                        wait(st, g, "v_ready", CUT[layer] + s + 1)
                    if i % HT == 0:
                        wait(st, g, selected, f + (SEL[layer] if s == 0 else 2 * NTH[layer] * (st is late)) + 1)
                    alone()
                    for j in range(NT):
                        for q in range(3):
                            last = nc.tensor.matmul(
                                st.mps[:, k % 2, s * E1:(s + 1) * E1], halves(st, f)[:, s, j, (i % HT) * P:(i % HT + 1) * P],
                                st.V1[:, j, q, s * E1:(s + 1) * E1], start=(j == 0 and q == 0),
                                stop=(j == NT - 1 and q == 2))
                last.then_inc(st.S["slot_full"], 1)

            def gproj(g):
                wait(late, g, "gen_free", USE[4]["T"] + 2)
                for f in range(2):
                    o = bank(g, 4, "proj", f)
                    for t in range(HT):
                        last = nc.tensor.matmul(o[:, t * P:(t + 1) * P], late.hT[:, (HT * f + t) * P:(HT * f + t + 1) * P],
                                                K1s[:, :], start=True, stop=True)
                    full(last, 4)

            def gagg(g, i):
                if i == 0:
                    wait(late, g, "v_ready", 5)
                    wait(prep, g, "a8_done", NT)
                k = SLOT[4] + i
                wait(late, g, "act_slot", k - 1)
                alone()
                for j in range(NT):
                    for q in range(3):
                        last = nc.tensor.matmul(late.mps[:, k % 2, 0:F], A8[:, g.par, j, i * P:(i + 1) * P],
                                                V3[:, j, q, :], start=(j == 0 and q == 0),
                                                stop=(j == NT - 1 and q == 2))
                last.then_inc(late.S["slot_full"], 1)

            def gstat(g):
                wait(late, g, "region", 1)
                o = bank(g, 4, "stats", 0)
                for s, src in ((0, region), (1, square)):
                    for t in range(NT):
                        last = nc.tensor.matmul(o[:, s:s + 1], src[:, t, :], ones[:, 0:1], start=(t == 0),
                                                stop=(t == NT - 1))
                full(last, 4)

            def gq(g):
                o = bank(g, 4, "q", 0)
                alone()
                for i in range(NT):
                    for j in range(NT):
                        last = nc.tensor.matmul(o[:, 3 * i:3 * i + 3], AT[:, g.par, j, i * P:(i + 1) * P],
                                                rc3[:, g.par, j, :], start=(j == 0), stop=(j == NT - 1))
                full(last, 4)

            def gout(g):
                wait(late, g, "v_ready", 6)
                for f in range(2):
                    o = bank(g, 4, "G", f)
                    alone()
                    for j in range(NT):
                        for q in range(3):
                            last = nc.tensor.matmul(o, V3[:, j, q, :], AT[:, g.par, j, f * HALF:(f + 1) * HALF],
                                                    start=(j == 0 and q == 0), stop=(j == NT - 1 and q == 2))
                    full(last, 4)

            pe.wait_ge(w_land, 16 * LOADS)
            pe.wait_ge(w_pool, 4)
            nc.tensor.transpose(early.gen[:, 0, 0:F], early.Hin[:, 0, :], ident[:, :]).then_inc(w_pe, 1)
            pe.wait_ge(w_dve, 17)
            run(pe, dict(tr=tr, lin=lin, proj=proj, rows=rows, mean=mean, mask=mask, head=head, slot=slot, gproj=gproj,
                         gagg=gagg, gstat=gstat, gq=gq, gout=gout))

            pe.wait_ge(t_chain, 1)
            nc.tensor.transpose(late.gen[0:B * NT, 0, 0:P], Qall[:, :], ident[:, :]).then_inc(t_peq, 1)
            pe.wait_ge(t_scale, 1)
            nc.tensor.matmul(early.gen[0:3, 0, 0:F], tcol, K2s[:, :], start=True, stop=True).then_inc(t_petk, 1)
            pe.wait_ge(t_tp, 1)
            pe.wait_ge(t_q, 48)
            for g in range(TG):
                if g % 4 == 0:
                    pe.wait_ge(t_gt[g // 4], 64)
                if g >= 4:
                    pe.wait_ge(t_kept, g - 3)
                nc.tensor.matmul(ring4[g % 4], K2n, GT[:, g * 512:(g + 1) * 512], start=True, stop=False)
                for a in range(3):
                    last = nc.tensor.matmul(ring4[g % 4], tK2p[:, a, :], qrow[:, g * 512:(g + 1) * 512],
                                            start=False, stop=(a == 2))
                last.then_inc(t_full, 1)
            for g in range(TG):
                pe.wait_ge(t_norm, 1 + g)
                if g >= 4:
                    pe.wait_ge(t_out, g - 3)
                for t in range(HT):
                    last = nc.tensor.transpose(ring4[g % 4][:, t * P:(t + 1) * P],
                                               GT[:, g * 512 + t * P:g * 512 + (t + 1) * P], ident[:, :])
                last.then_inc(t_back, 1)


def kernel(x, adj, L0_gnn_W1, L0_gnn_a1, L0_gnn_W2, L0_gnn_a2, L1_gnn_W, L1_gnn_a, L2_gnn_W, L2_gnn_a,
           L3_gnn_kernel_1, L3_gnn_bias_1, L3_gnn_gamma_1, L3_gnn_beta_1,
           L3_gnn_kernel_2, L3_gnn_bias_2, L3_gnn_gamma_2, L3_gnn_beta_2):
    import concourse.bacc as bacc
    import numpy as np
    from concourse.bass_utils import run_bass_kernel_spmd

    names = ["x", "adj", "L0_W1", "L0_a1", "L0_W2", "L0_a2", "L1_W", "L1_a", "L2_W", "L2_a", "L3_K1", "L3_b1",
             "L3_gamma1", "L3_beta1", "L3_K2", "L3_b2", "L3_gamma2", "L3_beta2"]
    given = [x, adj, L0_gnn_W1, L0_gnn_a1, L0_gnn_W2, L0_gnn_a2, L1_gnn_W, L1_gnn_a, L2_gnn_W, L2_gnn_a,
             L3_gnn_kernel_1, L3_gnn_bias_1, L3_gnn_gamma_1, L3_gnn_beta_1,
             L3_gnn_kernel_2, L3_gnn_bias_2, L3_gnn_gamma_2, L3_gnn_beta_2]
    nc = bacc.Bacc("TRN2", target_bir_lowering=False, num_devices=1)
    arrays, aps = {}, []
    for name, a in zip(names, given):
        a = np.ascontiguousarray(a)
        arrays["in_" + name] = a
        aps.append(nc.dram_tensor("in_" + name, a.shape, mybir.dt.from_np(a.dtype), kind="ExternalInput").ap())
    out = nc.dram_tensor("out_0", x.shape, F32, kind="ExternalOutput").ap()
    adjacency_gnn_stack(nc, *aps, out)
    got = run_bass_kernel_spmd(nc, [arrays], core_ids=[0])
    return got.results[0]["out_0"]
```
